# Optimizing a Trainium2 kernel written in Bass

```python
import numpy as np
import jax
import jax.numpy as jnp

def _softmax(x, axis=-1):
    return jax.nn.softmax(x, axis=axis)

def _gelu(x):
    return jax.nn.gelu(x, approximate=True)

def _silu(x):
    return jax.nn.silu(x)

def _sigmoid(x):
    return jax.nn.sigmoid(x)

def _layernorm(x, axis=-1, eps=1e-05):
    m = jnp.mean(x, axis=axis, keepdims=True)
    v = jnp.var(x, axis=axis, keepdims=True)
    return (x - m) / jnp.sqrt(v + eps)

def _scatter_add(tgt, idx, src, axis=0):
    return tgt.at[idx].add(src)

def _segment_sum(src, seg, n):
    return jax.ops.segment_sum(src, seg, n)
kernel_name = 'mk_lm_tower_d1_tok_ids512_r4_d8cc5d'

def setup_inputs(seed: int=0):
    np.random.seed(seed)
    _w = jnp.asarray

    def _rec_inputs():
        import jax
        import jax.numpy as jnp
        _rk = jax.random.key(seed)
        x = jax.random.randint(jax.random.fold_in(_rk, 1), (32, 256), 0, 125, jnp.int32)
        return x
    x = _rec_inputs()

    def _L0_tok_setup():
        import jax, jax.numpy as jnp
        import numpy as np
        VOCAB = 125
        DIM = 128
        CONTEXT = 2
        GROUPS = DIM // 4
        key = jax.random.key(seed)
        k1, k2, k3 = jax.random.split(key, 3)
        y = jax.random.randint(k1, (64, 512), 0, VOCAB, dtype=jnp.int64)
        emb_table = jax.random.normal(k2, (VOCAB, DIM), dtype=jnp.float32)
        conv_w = jax.random.normal(k3, (DIM, DIM // GROUPS, CONTEXT), dtype=jnp.float32) * 0.1
        return {'y': y, 'emb_table': emb_table, 'conv_w': conv_w}
    _L0_tok_all = _L0_tok_setup()
    _L0_tok_in = {k: v for k, v in _L0_tok_all.items() if k in ('emb_table', 'conv_w')}
    del _L0_tok_all

    def _L0_attn_setup():
        import jax, jax.numpy as jnp
        import numpy as np
        NUM_HEADS = 8
        WINDOW = 64
        key = jax.random.key(seed)
        k1, k2, k3, k4, k5 = jax.random.split(key, 5)
        B, T, D = (1, 1024, 128)
        x = jax.random.normal(k1, (B, T, D), dtype=jnp.float32)
        Wq = jax.random.normal(k2, (D, D), dtype=jnp.float32) * D ** (-0.5)
        Wk = jax.random.normal(k3, (D, D), dtype=jnp.float32) * D ** (-0.5)
        Wv = jax.random.normal(k4, (D, D), dtype=jnp.float32) * D ** (-0.5)
        rel_pos_bias = jax.random.normal(k5, (1, NUM_HEADS, 2 * WINDOW - 1), dtype=jnp.float32)
        return {'x': x, 'Wq': Wq, 'Wk': Wk, 'Wv': Wv, 'rel_pos_bias': rel_pos_bias}
    _L0_attn_all = _L0_attn_setup()
    _L0_attn_in = {k: v for k, v in _L0_attn_all.items() if k in ('Wq', 'Wk', 'Wv', 'rel_pos_bias')}
    del _L0_attn_all

    def _L0_ffn_setup():
        import jax, jax.numpy as jnp
        import numpy as np
        TOP_K = 2
        key = jax.random.key(seed)
        k1, k2, k3, k4 = jax.random.split(key, 4)
        B, S, D, F, E = (4, 128, 128, 512, 16)
        hidden_states = jax.random.normal(k1, (B, S, D), dtype=jnp.float32)
        gate_weight = jax.random.normal(k2, (E, D), dtype=jnp.float32) * 0.02
        w1 = jax.random.normal(k3, (E, F, D), dtype=jnp.float32) * 0.02
        w2 = jax.random.normal(k4, (E, D, F), dtype=jnp.float32) * 0.02
        return {'hidden_states': hidden_states, 'gate_weight': gate_weight, 'w1': w1, 'w2': w2}
    _L0_ffn_all = _L0_ffn_setup()
    _L0_ffn_in = {k: v for k, v in _L0_ffn_all.items() if k in ('gate_weight', 'w1', 'w2')}
    del _L0_ffn_all
    return {'x': x, 'L0_tok_emb_table': _L0_tok_in['emb_table'], 'L0_tok_conv_w': _L0_tok_in['conv_w'], 'L0_attn_Wq': _L0_attn_in['Wq'], 'L0_attn_Wk': _L0_attn_in['Wk'], 'L0_attn_Wv': _L0_attn_in['Wv'], 'L0_attn_rel_pos_bias': _L0_attn_in['rel_pos_bias'], 'L0_ffn_gate_weight': _L0_ffn_in['gate_weight'], 'L0_ffn_w1': _L0_ffn_in['w1'], 'L0_ffn_w2': _L0_ffn_in['w2']}

def reference(x, L0_tok_emb_table, L0_tok_conv_w, L0_attn_Wq, L0_attn_Wk, L0_attn_Wv, L0_attn_rel_pos_bias, L0_ffn_gate_weight, L0_ffn_w1, L0_ffn_w2):
    import jax
    import jax.numpy as jnp

    def _L0_tok_ref(y, emb_table, conv_w):
        import jax, jax.numpy as jnp
        import numpy as np
        VOCAB = 125
        DIM = 128
        CONTEXT = 2
        GROUPS = DIM // 4
        mask = y >= 0
        emb = emb_table[jnp.clip(y, 0)] * mask[..., None].astype(emb_table.dtype)
        x = jnp.transpose(emb, (0, 2, 1))
        x = jnp.pad(x, ((0, 0), (0, 0), (CONTEXT - 1, 0)))
        out = jax.lax.conv_general_dilated(x, conv_w, window_strides=(1,), padding='VALID', dimension_numbers=('NCH', 'OIH', 'NCH'), feature_group_count=GROUPS)
        out = jnp.transpose(out, (0, 2, 1))
        return jax.nn.relu(out)

    def _L0_attn_ref(x, Wq, Wk, Wv, rel_pos_bias):
        import jax, jax.numpy as jnp
        import numpy as np
        NUM_HEADS = 8
        WINDOW = 64
        B, T, D = x.shape
        H = NUM_HEADS
        hd = D // H
        scale = hd ** (-0.5)
        q = (x @ Wq.T).reshape(B, T, H, hd).transpose(0, 2, 1, 3)
        k = (x @ Wk.T).reshape(B, T, H, hd).transpose(0, 2, 1, 3)
        v = (x @ Wv.T).reshape(B, T, H, hd).transpose(0, 2, 1, 3)
        pos = jnp.arange(T)
        rel = jnp.clip(pos[:, None] - pos[None, :], -(WINDOW - 1), WINDOW - 1) + (WINDOW - 1)
        bias = rel_pos_bias[0][:, rel]
        scores = jnp.einsum('bhid,bhjd->bhij', q, k) * scale + bias[None]
        attn = jax.nn.softmax(scores, axis=-1)
        out = jnp.einsum('bhij,bhjd->bhid', attn, v)
        return out.transpose(0, 2, 1, 3).reshape(B, T, D)

    def _L0_ffn_ref(hidden_states, gate_weight, w1, w2):
        import jax, jax.numpy as jnp
        import numpy as np
        TOP_K = 2
        B, S, D = hidden_states.shape
        E = gate_weight.shape[0]
        x = hidden_states.reshape(-1, D)
        gate_logits = x @ gate_weight.T
        top_vals, top_idx = jax.lax.top_k(gate_logits, TOP_K)
        routing_w = jax.nn.softmax(top_vals, axis=-1)
        mask = jnp.any(top_idx[:, :, None] == jnp.arange(E)[None, None, :], axis=1)
        h = jax.nn.silu(jnp.einsum('td,efd->tef', x, w1))
        counts = jnp.sum(mask, axis=0)
        h_sum = jnp.einsum('tef,te->ef', h, mask.astype(h.dtype))
        h_mean = h_sum / jnp.maximum(counts, 1)[:, None].astype(h.dtype)
        y_mean = jnp.einsum('ef,edf->ed', h_mean, w2)
        y_mean = jnp.where((counts > 0)[:, None], y_mean, 0.0)
        out = jnp.einsum('tk,tkd->td', routing_w, y_mean[top_idx])
        return out.reshape(B, S, D)
    h = _L0_tok_ref(x, L0_tok_emb_table, L0_tok_conv_w)
    h = h + _L0_attn_ref(_layernorm(h, axis=-1), L0_attn_Wq, L0_attn_Wk, L0_attn_Wv, L0_attn_rel_pos_bias)
    h = h + _L0_ffn_ref(_layernorm(h, axis=-1), L0_ffn_gate_weight, L0_ffn_w1, L0_ffn_w2)
    return h

_drawn_inputs = setup_inputs


def setup_inputs(seed=0):
    import zlib

    import numpy as np

    out = dict(_drawn_inputs(seed))
    spreads = {}
    factors = {}
    for name, (base, spread) in spreads.items():
        noise = np.random.default_rng([zlib.crc32(name.encode()), seed]).standard_normal(out[name].shape)
        drawn = base * np.exp(spread * noise) if base else spread * noise
        out[name] = jnp.asarray(drawn.astype(out[name].dtype))
    for name, factor in factors.items():
        out[name] = (out[name] * factor).astype(out[name].dtype)
    return out
```

```python
from contextlib import ExitStack

import concourse.bass as bass
from concourse import mybir

F32 = mybir.dt.float32
BF16 = mybir.dt.bfloat16
I32 = mybir.dt.int32
U32 = mybir.dt.uint32
ALU = mybir.AluOpType
ACT = mybir.ActivationFunctionType
AX = mybir.AxisListType

P = 128
BATCH, T, D = 32, 256, 128
NT = T // P
TILES = BATCH * NT
H, HD = 8, 16
VW = 32
VOCAB, CONTEXT, GROUP = 125, 2, 4
WINDOW = 64
NREL = 2 * WINDOW - 1
BIASW = NT * P + P
E, F = 16, 512
TOP_K = 2
CAP = BATCH * T + P
ZERO_ROW = E * CAP
BLOCKS = -(-(BATCH * T * TOP_K // P + E - 1) // 8) * 8
UNROLL = 8
AHEAD = 2
EPS = 1e-5
TURNS = BLOCKS // UNROLL
LOW = -3.0e38
TERMS = [(0, 0), (0, 1), (1, 0), (1, 1), (0, 2), (2, 0)]
KROWS = len(TERMS) * HD
POOL_CONSTANTS, DVE_CONSTANTS = 23, 16
FIRST_STEP, LAST_STEP = -5, BATCH + 2


class Batch:
    def __init__(self, n):
        self.n = n
        self.par = n % 2
        self.quarter = n % 4
        self.half = n // 2
        self.live = 0 <= n < BATCH


def run_steps(eng, step):
    for s in range(FIRST_STEP, LAST_STEP + 1):
        step(lambda d: Batch(s + d))


def run_turns(eng, turn):
    turn(0)
    with eng.Fori(1, TURNS - 1) as i:
        turn(i)
    turn(TURNS - 1)


def wait(eng, semaphore, count):
    if not isinstance(count, int) or count > 0:
        eng.wait_ge(semaphore, count)


def tower_kernel(nc, x, emb, conv_w, wq, wk, wv, rel_bias, gate_w, w1, w2, out):
    with ExitStack() as ctx:
        def sb(name, shape, dt=F32):
            return ctx.enter_context(nc.sbuf_tensor(name, shape, dt))

        def pb(name, shape=(P, 512), dt=F32):
            return ctx.enter_context(nc.psum_tensor(name, list(shape), dt))

        def sem(name):
            return ctx.enter_context(nc.semaphore(name))

        expert_rows = nc.dram_tensor("expert_rows", (ZERO_ROW + P, D), F32)
        bias_rows = nc.dram_tensor("bias_rows", (H, 512), F32)

        ident = sb("ident", [P, P])
        identb = sb("identb", [P, P], BF16)
        anti = sb("anti", [P, P])
        onesf = sb("onesf", [P, P])
        onesb = sb("onesb", [P, P], BF16)
        earlier = sb("earlier", [P, P], BF16)
        minus_sel = sb("minus_sel", [P, H, P], BF16)
        group_mask = sb("group_mask", [P, P])
        tile_mask = sb("tile_mask", [P, 8])
        vocab_i = sb("vocab_i", [P, 1], I32)
        vocab_f = sb("vocab_f", [P, 1])
        expert_i = sb("expert_i", [P, E], I32)
        expert_f = sb("expert_f", [P, E])
        region = sb("region", [P, E])
        minus_half = sb("minus_half", [P, NT])
        zeros = sb("zeros", [P, P])
        w_nat = sb("w_nat", [P, 3, P])
        gate_nat = sb("gate_nat", [E, D])
        emb_nat = sb("emb_nat", [VOCAB, D])
        conv_nat = sb("conv_nat", [P, GROUP, CONTEXT])
        bias_t = sb("bias_t", [NREL, H])
        conv_wide = sb("conv_wide", [P, CONTEXT, P])
        wqkT = sb("wqkT", [P, 2, P])
        wvT = sb("wvT", [P, P])
        gateT = sb("gateT", [P, E])
        embT = sb("embT", [P, VOCAB])
        convT = sb("convT", [P, CONTEXT, P])
        table = sb("table", [P, CONTEXT, D])
        bias_ext = sb("bias_ext", [H, 512])
        arena = sb("arena", [P, E * F])
        stack_cols = 2 * H * T // 2
        stack = [arena[0:KROWS, i * stack_cols:(i + 1) * stack_cols].bitcast(BF16).rearrange(
            "p (s h t) -> p s h t", s=2, h=H) for i in range(2)]
        bias_at, full_at = 2 * stack_cols, 2 * stack_cols + H * BIASW
        bias_flat = arena[:, bias_at:full_at]
        bias = bias_flat.rearrange("p (h u) -> p h u", h=H)
        qk_full = [arena[:, full_at + i * 2 * T:full_at + (i + 1) * 2 * T].rearrange(
            "p (s t) -> p s t", s=2) for i in range(2)]
        w2_nat = arena[:, :].rearrange("p (e f) -> p e f", e=E)
        w1_in = [sb(f"w1_in{i}", [P, 2, D]) for i in range(2)]
        w1T = sb("w1T", [P, E * F])
        tok = [sb(f"tok{i}", [P, T], I32) for i in range(2)]
        onehot = [sb(f"onehot{i}", [P, 1 + T]) for i in range(2)]
        hres = sb("hres", [P, TILES, D])
        stats = [sb(f"stats{i}", [P, NT, 6]) for i in range(2)]
        moments = [sb(f"moments{i}", [P, NT, 2]) for i in range(2)]
        var_eps = [sb(f"var_eps{i}", [P, NT]) for i in range(2)]
        rstd = [sb(f"rstd{i}", [P, NT]) for i in range(2)]
        xn = [sb(f"xn{i}", [P, NT, D]) for i in range(2)]
        xnT = [sb(f"xnT{i}", [P, T]) for i in range(2)]
        qk_rest = sb("qk_rest", [P, 2, T])
        qk_part = [sb(f"qk_part{i}", [P, 2, 3, T], BF16) for i in range(2)]
        v_op = [sb(f"v_op{i}", [P, NT, H, VW]) for i in range(4)]
        scored = sb("scored", [P, 2, H, NT * T])
        row_max = [sb(f"row_max{i}", [P, NT, H]) for i in range(2)]
        max_parts = [sb(f"max_parts{i}", [P, NT, 2 * H], BF16) for i in range(2)]
        maxT = [sb(f"maxT{i}", [P, T], BF16) for i in range(2)]
        probs = sb("probs", [P, H, NT * T])
        oT = sb("oT", [P, 2 * T])
        o_rec = sb("o_rec", [P, NT * H])
        o_norm = sb("o_norm", [P, NT, D])
        stats2 = sb("stats2", [P, NT, 6])
        moments2 = sb("moments2", [P, NT, 2])
        var_eps2 = sb("var_eps2", [P, NT])
        rstd2 = sb("rstd2", [P, NT])
        xn2 = [sb(f"xn2_{i}", [P, NT, D]) for i in range(2)]
        xn2T = sb("xn2T", [P, T])
        logits = sb("logits", [P, NT, E])
        largest = sb("largest", [P, NT, 8])
        largest_at = sb("largest_at", [P, NT, 8], U32)
        chosen = [sb(f"chosen{i}", [P, TOP_K, NT, E]) for i in range(2)]
        mask = [sb(f"mask{i}", [P, NT, E], BF16) for i in range(2)]
        before = [sb(f"before{i}", [P, NT, E], BF16) for i in range(2)]
        slot = sb("slot", [P, NT, E])
        slot_of = sb("slot_of", [P, TOP_K, NT, E])
        slot_f = sb("slot_f", [P, TOP_K * NT])
        slot_i = [sb(f"slot_i{i}", [P, TOP_K * NT], I32) for i in range(2)]
        gap_all = sb("gap_all", [P, TILES])
        chosen_all = sb("chosen_all", [P, TOP_K, TILES, E], BF16)

        sums = scored[:, :, :, :].rearrange("p a h t -> p (a h t)")
        hidden = [probs[:, i, :] for i in range(2)]
        block_rows = [probs[:, 2, i * D:(i + 1) * D] for i in range(4)] + [
            xnT[i // 2][:, (i % 2) * D:(i % 2 + 1) * D] for i in range(4)]
        y_prod = [probs[:, 6 + i, :] for i in range(2)]
        blockT = [probs[:, 5, i * P:(i + 1) * P] for i in range(4)]
        counts = sb("counts", [P, E])
        counts1 = sb("counts1", [P, E])
        per_token = sb("per_token", [P, E])
        end_i = sb("end_i", [P, E], I32)
        blocks_i = sb("blocks_i", [P, E], I32)
        blocks_s = sb("blocks_s", [P, E], I32)
        blocks = sb("blocks", [P, E])
        block_end = sb("block_end", [P, E])
        block_k = sb("block_k", [P, 1])
        passed = sb("passed", [P, E])
        plan_e = sb("plan_e", [P, 1])
        plan_b = sb("plan_b", [P, 1])
        plan_l = sb("plan_l", [P, 1])
        plan_f = sb("plan_f", [P, 4])
        plan_i = sb("plan_i", [1, 4 * P], I32)
        gap_exp = sb("gap_exp", [P, TILES])
        gap_exp1 = sb("gap_exp1", [P, TILES])
        share = sb("share", [P, TOP_K, TILES])
        gates_k = probs[:, 4:8, :].rearrange("p a (k t e) -> p (a k) (t e)", k=1, e=E).rearrange(
            "p (k a) (t e) -> p k (a t) e", k=TOP_K, e=E)
        gates = sb("gates", [P, TILES, E])
        gateT_all = probs[:, 3:5, :].rearrange("p a (g t) -> p (a g) t", t=P)
        yT = sb("yT", [P, E])
        y_wide = w_nat[:, 0, :].rearrange("p (a e) -> p a e", a=8)
        y_block = gates[:, :, :].rearrange("p (t a) e -> p t (a e)", t=8)

        ps_score = [pb(f"ps_score{i}") for i in range(2)]
        ps_turn = [pb(f"ps_turn{i}") for i in range(2)]
        ps_val = pb("ps_val")
        bank_a, bank_b, bank_c = pb("bank_a"), pb("bank_b"), pb("bank_c")
        emb_ps, xnT_ps = bank_a[:, 0:T], bank_a[:, T:2 * T]
        v_ps, w1_ps = bank_a[:, 0:T], bank_a[:, T:2 * T]
        qk_ps = bank_b[:, :]
        o_ps = bank_b[:, :]
        xn2T_ps = bank_c[:, 0:T]
        max_ps = bank_c[0:2 * H, T:T + P].bitcast(BF16)
        logit_ps = bank_c[:, 384:384 + NT * E]
        rank_ps = bank_c[:, 416:416 + NT * E]

        up_ps = ps_score + ps_turn
        turn_ps = [bank[:, 0:P] for bank in (bank_a, bank_b, bank_c, ps_val)]

        names = """plan_done padded block_turned result_done stored sums_zero gap_exp_done gate_mm gateT_done up_mm
        summed silu_done plan_dve plan_ready plan_mm count_mm gates_done blockT_done spread_mm y_done y_wide_done y_mm
        y_block_done mix_mm weights_in small_in bias_in bias_row bias_wide const_pool const_dve setup_pe setup_dve table_done
        bias_ps bias_done w2_in zero_row_out onehot_done embed_mm relu_done stat_dve rstd_pool xn_done xnT_mm xnT_done
        w1_mm w1_done qk_mm part1_done full_done split_pool part2_done v_mm v_done scores_mm scored_dve
        max_split max_mm maxT_done turned_mm exp_done val_mm oT_done o_mm o_chain o_norm_done hres_done
        ln2_dve rstd2_pool xn2_done xn2T_mm xn2T_done logit_mm route_dve gap_done chosen_kept count_pool rank_mm slot_dve""".split()
        S = {n: sem(n) for n in names}
        tok_in = [sem(f"tok_in{i}") for i in range(2)]
        w1_loaded = [sem(f"w1_loaded{i}") for i in range(2)]
        scattered = [sem(f"scattered{i}") for i in range(2)]
        block_in = [sem(f"block_in{i}") for i in range(UNROLL)]
        stacked = [sem(f"stacked{i}") for i in range(2)]
        STAT, SPLIT, LN2, RSTD2, ROUTE, COUNT, SLOT = 4, 2, 4, 2, 8, 2, 4

        SP, PE, DVE = mybir.EngineType.SP, mybir.EngineType.PE, mybir.EngineType.DVE

        def plan_values(engine, at, largest_value):
            values = []
            for half in range(UNROLL // 4):
                _, four = nc.values_load_multi_w_load_instructions(
                    plan_i[0:1, bass.ds(at + 4 * half, 4)], engines=[engine], min_val=0, max_val=largest_value,
                    skip_runtime_bounds_check_because="the plan is made on the chip from counts and cut to this range")
                values += list(four)
            return values

        def route_logits(v, b):
            if b.live:
                v.wait_ge(S["logit_mm"], b.n + 1)
                v.tensor_copy(logits[:, :, :].rearrange("p t e -> p (t e)"), logit_ps).then_inc(S["route_dve"], 1)

        def route_largest(v, b):
            if b.live:
                v.wait_ge(S["route_dve"], ROUTE * b.n + 1)
                for t in range(NT):
                    v.max(largest[:, t, :], logits[:, t, :]).then_inc(S["route_dve"], 1)

        def route_index(v, b):
            if b.live:
                v.wait_ge(S["route_dve"], ROUTE * b.n + 1 + NT)
                for t in range(NT):
                    v.max_index(largest_at[:, t, :], largest[:, t, :], logits[:, t, :]).then_inc(S["route_dve"], 1)

        def route_choice(v, b):
            if b.live:
                v.wait_ge(S["route_dve"], ROUTE * b.n + 1 + 2 * NT)
                wait(v, S["chosen_kept"], b.n - 1)
                wait(v, S["slot_dve"], SLOT * b.n - SLOT)
                for k in range(TOP_K):
                    at = largest_at[:, :, k:k + 1].broadcast_to([P, NT, E])
                    ex = expert_f[:, :].unsqueeze(1).broadcast_to([P, NT, E])
                    v.tensor_tensor(chosen[b.par][:, k, :, :], ex, at, ALU.is_equal).then_inc(S["route_dve"], 1)
                v.tensor_tensor(gap_all[:, bass.ds(NT * b.n, NT)].unsqueeze(2), largest[:, :, 1:2],
                                largest[:, :, 0:1], ALU.subtract).then_inc(S["gap_done"], 1)

        def route_mask(v, b):
            if b.live:
                v.wait_ge(S["route_dve"], ROUTE * b.n + 1 + 2 * NT + TOP_K)
                v.wait_ge(S["gap_done"], b.n + 1)
                wait(v, S["rank_mm"], b.n - 1)
                wait(v, S["count_pool"], COUNT * b.n - COUNT)
                v.tensor_tensor(mask[b.par][:, :, :], chosen[b.par][:, 0, :, :], chosen[b.par][:, 1, :, :],
                                ALU.add).then_inc(S["route_dve"], 1)

        def place(v, b, stage):
            if not b.live:
                return
            if stage == 0:
                v.wait_ge(S["rank_mm"], b.n + 1)
                wait(v, S["slot_dve"], SLOT * b.n)
                v.tensor_tensor(slot[:, :, :], rank_ps.rearrange("p (t e) -> p t e", e=E),
                                region[:, :].unsqueeze(1).broadcast_to([P, NT, E]), ALU.add).then_inc(
                    S["slot_dve"], 1)
            if stage == 1:
                v.wait_ge(S["slot_dve"], SLOT * b.n + 1)
                v.tensor_tensor(slot_of[:, :, :, :], chosen[b.par][:, :, :, :],
                                slot[:, :, :].unsqueeze(1).broadcast_to([P, TOP_K, NT, E]), ALU.mult).then_inc(
                    S["slot_dve"], 1)
            if stage == 2:
                v.wait_ge(S["slot_dve"], SLOT * b.n + 2)
                v.tensor_reduce(slot_f[:, :], slot_of[:, :, :, :].rearrange("p k t e -> p (k t) e"), AX.X,
                                ALU.add).then_inc(S["slot_dve"], 1)
            if stage == 3:
                v.wait_ge(S["slot_dve"], SLOT * b.n + 3)
                wait(v, scattered[b.par], 16 * TOP_K * NT * b.half)
                v.tensor_copy(slot_i[b.par][:, :], slot_f[:, :]).then_inc(S["slot_dve"], 1)

        def finish_sync(sp):
            for i in range(2):
                sp.wait_ge(scattered[i], 16 * TOP_K * TILES // 2)
            sp.wait_ge(S["plan_done"], 1)
            with sp.Fori(0, E) as e:
                end = sp.value_load(end_i[0:1, bass.ds(e, 1)], min_val=0, max_val=ZERO_ROW - P)
                sp.dma_start(expert_rows[bass.ds(end, P), :], zeros[:, :]).then_inc(S["padded"], 16)
            sp.wait_ge(S["zero_row_out"], 16)
            sp.wait_ge(S["padded"], 16 * E)
            sp.wait_ge(S["val_mm"], 2 * BATCH)
            sp.wait_ge(S["plan_done"], 2)

            def load(turn):
                rows = plan_values(SP, UNROLL * turn, ZERO_ROW)
                for u, row in enumerate(rows):
                    wait(sp, S["block_turned"], UNROLL * turn + u - UNROLL + 1)
                    sp.dma_start(block_rows[u], expert_rows[bass.ds(row, P), :]).then_inc(block_in[u], 16)

            run_turns(sp, load)
            out_v = out.rearrange("b (t p) d -> p (b t) d", p=P)
            for i in range(TILES // 4):
                sp.wait_ge(S["result_done"], i + 1)
                sp.dma_start(out_v[:, 4 * i:4 * i + 4, :], hres[:, 4 * i:4 * i + 4, :]).then_inc(S["stored"], 16)
            sp.wait_ge(S["stored"], 16 * (TILES // 4))

        def finish_gpsimd(g):
            g.wait_ge(S["scored_dve"], NT * H * BATCH)
            g.dma_start(w2_nat[:, :, :], w2.rearrange("e d f -> d e f")).then_inc(S["w2_in"], 16)
            g.wait_ge(S["turned_mm"], H * BATCH)
            g.memset(sums[:, E * F // 2:E * F], 0.0).then_inc(S["sums_zero"], 1)

        def finish_scalar(act):
            act.wait_ge(S["gap_done"], BATCH)
            act.activation(gap_exp[:, :], gap_all[:, :], ACT.Exp).then_inc(S["gap_exp_done"], 1)
            for i, bank in enumerate((bank_a, bank_b)):
                act.wait_ge(S["gate_mm"], i + 1)
                act.copy(gateT_all[:, 4 * i:4 * i + 4, :].rearrange("p g t -> p (g t)"), bank[:, :]).then_inc(
                    S["gateT_done"], 1)

            def copy_rows(k, u):
                act.wait_ge(S["block_turned"], k + 1)
                act.copy(blockT[u % 4], turn_ps[u % 4]).then_inc(S["blockT_done"], 1)

            def silu(k, u):
                act.wait_ge(S["up_mm"], k + 1)
                wait(act, S["summed"], k - 1)
                act.activation(hidden[u % 2], up_ps[u % 4][:, :], ACT.Silu).then_inc(S["silu_done"], 1)

            for u in range(AHEAD):
                copy_rows(u, u)

            def turn_of_blocks(turn):
                for u in range(UNROLL):
                    if not isinstance(turn, int) or turn < TURNS - 1 or u < UNROLL - AHEAD:
                        copy_rows(UNROLL * turn + u + AHEAD, u + AHEAD)
                    silu(UNROLL * turn + u, u)

            run_turns(act, turn_of_blocks)

        def finish_vector(v):
            done = 0

            def link(ins):
                nonlocal done
                done += 1
                ins.then_inc(S["plan_dve"], 1)
                v.wait_ge(S["plan_dve"], done)

            v.wait_ge(S["count_mm"], 1)
            link(v.tensor_copy(counts[:, :], bank_c[:, 0:E]))
            v.tensor_tensor(end_i[:, :], counts[:, :], region[:, :], ALU.add).then_inc(S["plan_done"], 1)
            link(v.tensor_scalar(blocks_i[:, :], counts[:, :], float(P - 1), None, ALU.add))
            link(v.tensor_single_scalar(blocks_s[:, :], blocks_i[:, :], 7, ALU.arith_shift_right))
            link(v.tensor_copy(blocks[:, :], blocks_s[:, :]))
            link(v.tensor_tensor_scan(block_end[:, :], onesf[:, 0:E], blocks[:, :], 0.0, ALU.mult, ALU.add))
            for c in range(2):
                link(v.tensor_scalar(block_k[:, :], vocab_f[:, :], float(P * c), None, ALU.add))
                link(v.tensor_scalar(passed[:, :], block_end[:, :], block_k[:, 0:1], None, ALU.is_le))
                link(v.tensor_reduce(plan_e[:, :], passed[:, :], AX.X, ALU.add))
                link(v.tensor_tensor(passed[:, :], passed[:, :], blocks[:, :], ALU.mult))
                link(v.tensor_reduce(plan_b[:, :], passed[:, :], AX.X, ALU.add))
                link(v.tensor_tensor(plan_b[:, :], block_k[:, :], plan_b[:, :], ALU.subtract))
                link(v.tensor_scalar(plan_l[:, :], plan_e[:, :], float(E), float(P), ALU.is_lt, ALU.mult))
                link(v.tensor_tensor(plan_b[:, :], plan_b[:, :], plan_l[:, :], ALU.mult))
                link(v.scalar_tensor_tensor(out=plan_f[:, c:c + 1], in0=plan_e[:, :], scalar=float(CAP),
                                            in1=plan_b[:, :], op0=ALU.mult, op1=ALU.add))
                link(v.tensor_scalar(plan_f[:, 2 + c:3 + c], plan_e[:, :], float(E - 1), float(F), ALU.min,
                                     ALU.mult))
            v.sem_inc(S["plan_ready"], 1)
            v.wait_ge(S["plan_mm"], 1)
            v.tensor_copy(plan_i[:, :], bank_c[0:1, :]).then_inc(S["plan_done"], 1)
            v.wait_ge(S["turned_mm"], H * BATCH)
            v.memset(sums[:, 0:E * F // 2], 0.0).then_inc(S["sums_zero"], 1)
            v.wait_ge(S["gap_exp_done"], 1)
            v.wait_ge(S["chosen_kept"], BATCH)
            v.wait_ge(S["val_mm"], 2 * BATCH)
            link(v.tensor_scalar(gap_exp1[:, :], gap_exp[:, :], 1.0, None, ALU.add))
            link(v.reciprocal(share[:, 0, :], gap_exp1[:, :]))
            link(v.tensor_tensor(share[:, 1, :], gap_exp[:, :], share[:, 0, :], ALU.mult))
            for k in range(TOP_K):
                link(v.tensor_tensor(gates_k[:, k, :, :], chosen_all[:, k, :, :],
                                     share[:, k, :].unsqueeze(2).broadcast_to([P, TILES, E]), ALU.mult))
            v.tensor_tensor(gates[:, :, :], gates_k[:, 0, :, :], gates_k[:, 1, :, :], ALU.add).then_inc(
                S["gates_done"], 1)

            v.wait_ge(S["plan_done"], 2)
            v.wait_ge(S["sums_zero"], 2)

            def add_hidden(turn):
                places = plan_values(DVE, 2 * P + UNROLL * turn, (E - 1) * F)
                for u, at in enumerate(places):
                    v.wait_ge(S["silu_done"], UNROLL * turn + u + 1)
                    wait(v, S["summed"], UNROLL * turn + u)
                    here = sums[:, bass.ds(at, F)]
                    v.tensor_tensor(here, here, hidden[u % 2], ALU.add).then_inc(S["summed"], 1)

            run_turns(v, add_hidden)
            v.wait_ge(S["w2_in"], 16)
            for e in range(E):
                v.wait_ge(S["spread_mm"], e + 1)
                wait(v, S["y_done"], e - 1)
                v.tensor_tensor_reduce(y_prod[e % 2], up_ps[e % 4][:, :], w2_nat[:, e, :], 1.0, 0.0, ALU.mult,
                                       ALU.add, yT[:, e:e + 1]).then_inc(S["y_done"], 1)
            v.wait_ge(S["y_done"], E)
            link(v.tensor_scalar(counts1[:, :], counts[:, :], 1.0, None, ALU.max))
            link(v.reciprocal(per_token[:, :], counts1[:, :]))
            v.tensor_tensor(y_wide[:, :, :], yT[:, :].unsqueeze(1).broadcast_to([P, 8, E]),
                            per_token[:, :].unsqueeze(1).broadcast_to([P, 8, E]), ALU.mult).then_inc(S["y_wide_done"], 1)
            v.wait_ge(S["y_mm"], 1)
            v.tensor_tensor(y_block[:, :, :], bank_c[:, 0:P].unsqueeze(1).broadcast_to([P, 8, D]),
                            tile_mask[:, :].unsqueeze(2).broadcast_to([P, 8, D]), ALU.mult).then_inc(
                S["y_block_done"], 1)
            for i in range(TILES // 4):
                v.wait_ge(S["mix_mm"], i + 1)
                here = hres[:, 4 * i:4 * i + 4, :].rearrange("p t d -> p (t d)")
                v.tensor_tensor(here, here, up_ps[i % 4][:, :], ALU.add).then_inc(S["result_done"], 1)

        def finish_tensor(pe):
            pe.wait_ge(S["count_pool"], COUNT * BATCH)
            pe.wait_ge(S["slot_dve"], SLOT * BATCH)
            pe.matmul(bank_c[:, 0:E], onesb[:, :], before[BATCH % 2][:, 0, :], start=True, stop=True).then_inc(
                S["count_mm"], 1)
            pe.wait_ge(S["plan_ready"], 1)
            for c in range(4):
                mm = pe.transpose(bank_c[0:1, c * P:(c + 1) * P], plan_f[:, c:c + 1], ident[:, :])
            mm.then_inc(S["plan_mm"], 1)
            pe.wait_ge(S["gates_done"], 1)
            pe.wait_ge(S["v_done"], BATCH)
            pe.wait_ge(S["w1_done"], BATCH)
            pe.wait_ge(S["o_norm_done"], BATCH)
            for g in range(8):
                mm = pe.transpose((bank_a, bank_b)[g // 4][:, (g % 4) * P:(g % 4 + 1) * P],
                                  gates[:, 8 * g:8 * g + 8, :].rearrange("p t e -> p (t e)"), ident[:, :])
                if g % 4 == 3:
                    mm.then_inc(S["gate_mm"], 1)
            pe.wait_ge(S["plan_done"], 2)
            pe.wait_ge(S["gateT_done"], 2)
            pe.wait_ge(S["exp_done"], H * BATCH)

            def turn_rows(turn, u):
                pe.wait_ge(block_in[u], 16 * turn + 16)
                pe.transpose(turn_ps[u % 4], block_rows[u], ident[:, :]).then_inc(S["block_turned"], 1)

            def products(turn):
                for u, at in enumerate(plan_values(PE, 2 * P + UNROLL * turn, (E - 1) * F)):
                    k = UNROLL * turn + u
                    if u < UNROLL - AHEAD:
                        turn_rows(turn, u + AHEAD)
                    elif not isinstance(turn, int) or turn < TURNS - 1:
                        turn_rows(turn + 1, u + AHEAD - UNROLL)
                    pe.wait_ge(S["blockT_done"], k + 1)
                    wait(pe, S["silu_done"], k - 3)
                    pe.matmul(up_ps[u % 4][:, :], blockT[u % 4], w1T[:, bass.ds(at, F)], start=True,
                              stop=True).then_inc(S["up_mm"], 1)

            for u in range(AHEAD):
                turn_rows(0, u)
            run_turns(pe, products)
            pe.wait_ge(S["summed"], BLOCKS)
            for e in range(E):
                wait(pe, S["y_done"], e - 3)
                pe.matmul(up_ps[e % 4][:, :], onesf[:, :], sums[:, e * F:(e + 1) * F], start=True,
                          stop=True).then_inc(S["spread_mm"], 1)
            pe.wait_ge(S["y_wide_done"], 1)
            pe.transpose(bank_c[:, 0:P], y_wide[:, :, :].rearrange("p t e -> p (t e)"), ident[:, :]).then_inc(
                S["y_mm"], 1)
            pe.wait_ge(S["y_block_done"], 1)
            pe.wait_ge(S["gateT_done"], 2)
            for i in range(TILES // 4):
                wait(pe, S["result_done"], i - 3)
                pe.matmul(up_ps[i % 4][:, :], gateT_all[:, i // 2, :],
                          y_block[:, 4 * (i % 2):4 * (i % 2) + 4, :].rearrange("p t d -> p (t d)"), start=True,
                          stop=True).then_inc(S["mix_mm"], 1)

        block = ctx.enter_context(nc.Block())

        @block.sync
        def _(sp):
            sp.dma_start(w_nat[:, 0, :], wq).then_inc(S["weights_in"], 16)
            sp.dma_start(w_nat[:, 1, :], wk).then_inc(S["weights_in"], 16)
            sp.dma_start(w_nat[:, 2, :], wv).then_inc(S["weights_in"], 16)
            sp.dma_start(gate_nat[:, :], gate_w).then_inc(S["weights_in"], 16)
            sp.dma_start(emb_nat[:, :], emb).then_inc(S["weights_in"], 16)
            sp.dma_start(conv_nat[:, :, :], conv_w).then_inc(S["small_in"], 16)
            with nc.allow_non_contiguous_dma(reason="a 4 KB table, once"):
                sp.dma_start(bias_t[:, :], rel_bias[0].rearrange("h r -> r h")).then_inc(S["small_in"], 16)
            sp.wait_ge(S["bias_row"], 3)
            sp.dma_start(bias_rows[:, :], bias_ext[:, :]).then_inc(S["bias_in"], 16)
            sp.wait_ge(S["bias_in"], 16)
            shifted = bass.AP(bias_rows, 0, [[1, P], [512, H], [1, BIASW]])
            sp.dma_start(probs[:, :, 0:BIASW], shifted).then_inc(S["bias_wide"], 16)

            def step(at):
                b = at(5)
                if b.live:
                    wait(sp, S["onehot_done"], b.n - 1)
                    row = x[bass.ds(b.n, 1), :]
                    sp.dma_start(tok[b.par][:, :], row.partition_broadcast(P)).then_inc(tok_in[b.par], 16)
                    wait(sp, S["w1_mm"], b.n - 1)
                    rows = w1.rearrange("e f d -> (e f) d")[bass.ds(b.n * 2 * P, 2 * P), :]
                    sp.dma_start(w1_in[b.par][:, :, :], rows.rearrange("(t p) d -> p t d", p=P)).then_inc(
                        w1_loaded[b.par], 16)
                b = at(3)
                if b.live:
                    sp.wait_ge(S["split_pool"], SPLIT * b.n + SPLIT)
                    sp.wait_ge(S["part2_done"], b.n + 1)
                    wait(sp, S["scores_mm"], H * b.n - H)
                    for i, (pq, pk) in enumerate(TERMS):
                        for side, part in ((0, pq), (1, pk)):
                            sp.dma_start(stack[b.par][i * HD:(i + 1) * HD, side, :, :],
                                         qk_part[b.par][:, side, part, :]).then_inc(stacked[b.par], 16)

            run_steps(sp, step)
            finish_sync(sp)

        @block.gpsimd
        def _(g):
            done = 0

            def tick(ins):
                nonlocal done
                done += 1
                ins.then_inc(S["const_pool"], 1)

            def made():
                g.wait_ge(S["const_pool"], done)

            tick(g.memset(ident[:, :], 0.0))
            tick(g.memset(identb[:, :], 0.0))
            tick(g.memset(anti[:, :], 0.0))
            tick(g.memset(group_mask[:, :], 1.0))
            made()
            diag = dict(compare_op=ALU.not_equal, fill=1.0, base=0, pattern=[[-1, P]], channel_multiplier=1)
            tick(g.affine_select(out=ident[:, :], in_=ident[:, :], **diag))
            tick(g.affine_select(out=identb[:, :], in_=identb[:, :], **diag))
            tick(g.affine_select(out=anti[:, :], in_=anti[:, :], compare_op=ALU.not_equal, fill=1.0,
                                 base=-(P - 1), pattern=[[1, P]], channel_multiplier=1))
            tick(g.affine_select(out=group_mask[:, :], in_=group_mask[:, :], compare_op=ALU.is_ge, fill=0.0,
                                 base=0, pattern=[[-GROUP, P // GROUP], [0, GROUP]], channel_multiplier=1))
            made()
            tick(g.affine_select(out=group_mask[:, :], in_=group_mask[:, :], compare_op=ALU.is_ge, fill=0.0,
                                 base=GROUP - 1, pattern=[[GROUP, P // GROUP], [0, GROUP]], channel_multiplier=-1))
            tick(g.iota(vocab_i[:, :], pattern=[[0, 1]], base=0, channel_multiplier=1))
            tick(g.iota(expert_i[:, :], pattern=[[1, E]], base=0, channel_multiplier=0))
            tick(g.memset(minus_half[:, :], -0.5))
            tick(g.memset(earlier[:, :], 1.0))
            tick(g.memset(minus_sel[:, :, :], 0.0))
            tick(g.memset(tile_mask[:, :], 1.0))
            made()
            tick(g.affine_select(out=minus_sel[:, :, :], in_=minus_sel[:, :, :], compare_op=ALU.not_equal,
                                 fill=-1.0, base=0, pattern=[[-1, H], [0, P]], channel_multiplier=1))
            tick(g.tensor_copy(vocab_f[:, :], vocab_i[:, :]))
            tick(g.tensor_copy(expert_f[:, :], expert_i[:, :]))
            tick(g.affine_select(out=earlier[:, :], in_=earlier[:, :], compare_op=ALU.is_gt, fill=0.0,
                                 base=0, pattern=[[1, P]], channel_multiplier=-1))
            tick(g.affine_select(out=tile_mask[:, :], in_=tile_mask[:, :], compare_op=ALU.is_ge, fill=0.0,
                                 base=0, pattern=[[-E, 8]], channel_multiplier=1))
            made()
            tick(g.affine_select(out=minus_sel[:, :, :], in_=minus_sel[:, :, :], compare_op=ALU.not_equal,
                                 fill=-1.0, base=-H, pattern=[[-1, H], [0, P]], channel_multiplier=1))
            tick(g.affine_select(out=tile_mask[:, :], in_=tile_mask[:, :], compare_op=ALU.is_ge, fill=0.0,
                                 base=E - 1, pattern=[[E, 8]], channel_multiplier=-1))
            tick(g.tensor_scalar(region[:, :], expert_f[:, :], float(CAP), None, ALU.mult))
            made()
            assert done == POOL_CONSTANTS
            g.wait_ge(S["const_dve"], DVE_CONSTANTS)
            g.dma_start(expert_rows[ZERO_ROW:ZERO_ROW + P, :], zeros[:, :]).then_inc(S["zero_row_out"], 16)

            def step(at):
                b = at(0)
                if b.live:
                    g.wait_ge(S["scored_dve"], NT * H * b.n + NT * H)
                    wait(g, S["max_mm"], b.n - 1)
                    m, parts = row_max[b.par], max_parts[b.par]
                    g.tensor_copy(parts[:, :, 0:H], m[:, :, :]).then_inc(S["max_split"], 1)
                    g.wait_ge(S["max_split"], 2 * b.n + 1)
                    g.tensor_tensor(parts[:, :, H:2 * H], m[:, :, :], parts[:, :, 0:H], ALU.subtract).then_inc(
                        S["max_split"], 1)
                b = at(4)
                if b.live:
                    g.wait_ge(S["stat_dve"], STAT * b.n + STAT)
                    g.tensor_scalar(var_eps[b.par][:, :], moments[b.par][:, :, 1], EPS, None, ALU.add).then_inc(
                        S["rstd_pool"], 1)
                    g.wait_ge(S["rstd_pool"], 2 * b.n + 1)
                    g.tensor_tensor(rstd[b.par][:, :], var_eps[b.par][:, :], minus_half[:, :], ALU.pow).then_inc(
                        S["rstd_pool"], 1)
                b = at(3)
                if b.live:
                    full, part = qk_full[b.par], qk_part[b.par]
                    g.wait_ge(S["part1_done"], b.n + 1)
                    g.wait_ge(S["full_done"], b.n + 1)
                    wait(g, S["split_pool"], SPLIT * b.n)
                    g.tensor_tensor(qk_rest[:, :, :], full[:, :, :], part[:, :, 0, :], ALU.subtract).then_inc(
                        S["split_pool"], 1)
                    g.wait_ge(S["part2_done"], b.n + 1)
                    g.tensor_tensor(part[:, :, 2, :], qk_rest[:, :, :], part[:, :, 1, :], ALU.subtract).then_inc(
                        S["split_pool"], 1)
                b = at(-2)
                if b.live:
                    g.wait_ge(S["route_dve"], ROUTE * b.n + ROUTE)
                    keep = chosen_all[:, :, bass.ds(NT * b.n, NT), :]
                    g.tensor_copy(keep, chosen[b.par][:, :, :, :]).then_inc(S["chosen_kept"], 1)
                    wait(g, S["rank_mm"], b.n)
                    wait(g, S["count_pool"], COUNT * b.n)
                    cur, nxt, m = before[b.par], before[1 - b.par], mask[b.par]
                    g.tensor_tensor(cur[:, 1, :], cur[:, 0, :], m[:, 0, :], ALU.add).then_inc(S["count_pool"], 1)
                    g.wait_ge(S["count_pool"], COUNT * b.n + 1)
                    g.tensor_tensor(nxt[:, 0, :], cur[:, 1, :], m[:, 1, :], ALU.add).then_inc(S["count_pool"], 1)
                b = at(-1)
                if b.live:
                    g.wait_ge(S["ln2_dve"], LN2 * b.n + LN2)
                    g.tensor_scalar(var_eps2[:, :], moments2[:, :, 1], EPS, None, ALU.add).then_inc(S["rstd2_pool"], 1)
                    g.wait_ge(S["rstd2_pool"], RSTD2 * b.n + 1)
                    g.tensor_tensor(rstd2[:, :], var_eps2[:, :], minus_half[:, :], ALU.pow).then_inc(
                        S["rstd2_pool"], 1)
                b = at(-3)
                if b.live:
                    g.wait_ge(S["slot_dve"], SLOT * b.n + SLOT)
                    for k in range(TOP_K):
                        for t in range(NT):
                            c = k * NT + t
                            g.indirect_dma_start(expert_rows[0:ZERO_ROW, :],
                                                 bass.IndirectOffsetOnAxis(slot_i[b.par][:, c:c + 1], 0),
                                                 xn2[b.par][:, t, :], None).then_inc(scattered[b.par], 16)

            run_steps(g, step)
            finish_gpsimd(g)

        @block.scalar
        def _(act):
            flat = bias_flat
            for i in range(1, 6, 2):
                act.wait_ge(S["bias_ps"], i + 1)
                bank = (bank_a, bank_b, bank_c)[i % 3]
                act.copy(flat[:, i * 512:(i + 1) * 512], bank[:, :]).then_inc(S["bias_done"], 1)

            def step(at):
                def exp(b, h):
                    if b.live:
                        act.wait_ge(S["turned_mm"], H * b.n + h + 1)
                        wait(act, S["val_mm"], 2 * b.n - 1 + h // 4)
                        act.activation(probs[:, h, :], ps_turn[h % 2][:, :], ACT.Exp).then_inc(S["exp_done"], 1)

                exp(at(-1), 6)
                b = at(4)
                if b.live:
                    act.wait_ge(S["embed_mm"], b.n + 1)
                    if at(3).live:
                        act.wait_ge(S["xnT_mm"], at(3).n + 1)
                    h = hres[:, bass.ds(NT * b.n, NT), :].rearrange("p t d -> p (t d)")
                    act.activation(h, emb_ps, ACT.Relu).then_inc(S["relu_done"], 1)
                b = at(3)
                if b.live:
                    act.wait_ge(S["xnT_mm"], b.n + 1)
                    wait(act, S["v_mm"], b.n - 1)
                    act.copy(xnT[b.par][:, :], xnT_ps).then_inc(S["xnT_done"], 1)
                b = at(0)
                if b.live:
                    act.wait_ge(S["max_mm"], b.n + 1)
                    wait(act, S["turned_mm"], H * b.n - H)
                    act.copy(maxT[b.par][0:2 * H, :], max_ps).then_inc(S["maxT_done"], 1)
                exp(at(-1), 7)
                b = at(3)
                if b.live:
                    act.wait_ge(S["qk_mm"], b.n + 1)
                    wait(act, stacked[b.par], 32 * len(TERMS) * b.half)
                    act.copy(qk_part[b.par][:, :, 0, :], qk_ps.rearrange("p (s t) -> p s t", s=2)).then_inc(
                        S["part1_done"], 1)
                exp(at(0), 0)
                exp(at(0), 1)
                b = at(-1)
                if b.live:
                    act.wait_ge(S["val_mm"], 2 * b.n + 2)
                    wait(act, S["o_mm"], b.n)
                    act.copy(oT[:, :], ps_val[:, :]).then_inc(S["oT_done"], 1)
                b = at(4)
                exp(at(0), 2)
                if b.live:
                    act.wait_ge(S["w1_mm"], b.n + 1)
                    act.copy(w1T[:, bass.ds(2 * P * b.n, 2 * P)], w1_ps).then_inc(S["w1_done"], 1)
                exp(at(0), 3)
                b = at(3)
                if b.live:
                    act.wait_ge(S["split_pool"], SPLIT * b.n + 1)
                    act.copy(qk_part[b.par][:, :, 1, :], qk_rest[:, :, :]).then_inc(S["part2_done"], 1)
                b = at(3)
                if b.live:
                    act.wait_ge(S["v_mm"], b.n + 1)
                    wait(act, S["val_mm"], 2 * b.n - 6)
                    act.copy(v_op[b.quarter][:, :, :, 0:HD],
                             v_ps.rearrange("p (t h d) -> p t h d", t=NT, d=HD)).then_inc(S["v_done"], 1)
                exp(at(0), 4)
                exp(at(0), 5)

            run_steps(act, step)
            finish_scalar(act)

        @block.vector
        def _(v):
            v.memset(zeros[:, :], 0.0).then_inc(S["const_dve"], 1)
            v.memset(onesf[:, :], 1.0).then_inc(S["const_dve"], 1)
            v.memset(onesb[:, :], 1.0).then_inc(S["const_dve"], 1)
            for i in range(4):
                v.memset(v_op[i][:, :, :, HD + 1:VW], 0.0).then_inc(S["const_dve"], 1)
                v.memset(v_op[i][:, :, :, HD:HD + 1], 1.0).then_inc(S["const_dve"], 1)
            for i in range(2):
                v.memset(maxT[i][:, :], 0.0).then_inc(S["const_dve"], 1)
                v.memset(onehot[i][:, 0:1], 0.0).then_inc(S["const_dve"], 1)
            v.memset(before[0][:, 0, :], 0.0).then_inc(S["const_dve"], 1)
            v.wait_ge(S["small_in"], 32)
            v.wait_ge(S["const_pool"], POOL_CONSTANTS)
            for k in range(CONTEXT):
                tap = conv_nat[:, :, k].unsqueeze(1).broadcast_to([P, P // GROUP, GROUP])
                v.tensor_tensor(conv_wide[:, k, :].rearrange("p (g c) -> p g c", c=GROUP),
                                group_mask[:, :].rearrange("p (g c) -> p g c", c=GROUP), tap, ALU.mult).then_inc(
                    S["setup_dve"], 1)
            v.wait_ge(S["setup_pe"], 1)
            for i in range(2):
                v.tensor_scalar(wqkT[:, i, :].rearrange("p (d h) -> p d h", h=H),
                                bank_a[:, i * P:(i + 1) * P].rearrange("p (h d) -> p d h", h=H),
                                HD ** -0.5 if i == 0 else 1.0, None, ALU.mult).then_inc(S["setup_dve"], 1)
            v.tensor_copy(wvT[:, :], bank_a[:, 2 * P:3 * P]).then_inc(S["setup_dve"], 1)
            v.tensor_copy(gateT[:, :], bank_a[:, 3 * P:3 * P + E]).then_inc(S["setup_dve"], 1)
            v.tensor_copy(embT[:, :], bank_b[:, 0:VOCAB]).then_inc(S["setup_dve"], 1)
            v.tensor_copy(convT[:, :, :], bank_b[:, P:3 * P].rearrange("p (k o) -> p k o", k=CONTEXT)).then_inc(
                S["setup_dve"], 1)
            v.wait_ge(S["setup_pe"], 2)
            v.tensor_copy(table[0:VOCAB, :, :], bank_c[0:VOCAB, 0:2 * D].rearrange("p (k o) -> p k o", k=CONTEXT)
                          ).then_inc(S["table_done"], 1)
            rev = bank_c[0:H, 2 * D:2 * D + NREL]
            lead = 2 * P - WINDOW
            v.tensor_copy(bias_ext[:, lead:lead + NREL], rev).then_inc(S["bias_row"], 1)
            v.tensor_copy(bias_ext[:, 0:lead], rev[:, 0:1].broadcast_to([H, lead])).then_inc(S["bias_row"], 1)
            tail = 512 - lead - NREL
            v.tensor_copy(bias_ext[:, 512 - tail:512], rev[:, NREL - 1:NREL].broadcast_to([H, tail])).then_inc(
                S["bias_row"], 1)
            flat = bias_flat
            for i in range(0, 6, 2):
                v.wait_ge(S["bias_ps"], i + 1)
                bank = (bank_a, bank_b, bank_c)[i % 3]
                v.tensor_copy(flat[:, i * 512:(i + 1) * 512], bank[:, :]).then_inc(S["bias_done"], 1)
            v.wait_ge(S["bias_done"], 6)

            def step(at):
                def score(h, t):
                    b = at(1)
                    if b.live:
                        if t == 0:
                            v.wait_ge(S["scores_mm"], H * b.n + h + 1)
                            wait(v, S["turned_mm"], H * b.n - 2 * H + h + 1)
                            if h == 0:
                                wait(v, S["max_split"], 2 * b.n - 2)
                        u = P - P * t
                        v.tensor_tensor_reduce(scored[:, b.par, h, t * T:(t + 1) * T],
                                               ps_score[h % 2][:, t * T:(t + 1) * T], bias[:, h, u:u + T],
                                               1.0, LOW, ALU.add, ALU.max,
                                               row_max[b.par][:, t, h:h + 1]).then_inc(S["scored_dve"], 1)

                def tile_of(b, t):
                    return hres[:, bass.ds(NT * b.n + t, 1), :].rearrange("p t d -> p (t d)")

                score(0, 0)
                place(v, at(-3), 0)
                score(0, 1)
                b = at(4)
                if b.live:
                    v.wait_ge(tok_in[b.par], 16 * b.half + 16)
                    wait(v, S["embed_mm"], b.n - 1)
                    v.tensor_scalar(onehot[b.par][:, 1:1 + T], tok[b.par][:, :], float(VOCAB - 1), vocab_f[:, 0:1],
                                    ALU.min, ALU.is_equal).then_inc(S["onehot_done"], 1)
                place(v, at(-3), 1)
                score(1, 0)
                place(v, at(-3), 2)
                score(1, 1)
                place(v, at(-3), 3)
                score(2, 0)
                score(2, 1)
                b = at(3)
                if b.live:
                    v.wait_ge(S["part1_done"], b.n + 1)
                    wait(v, S["split_pool"], SPLIT * b.n - SPLIT)
                    v.tensor_copy(qk_full[b.par][:, :, :].rearrange("p s t -> p (s t)"), qk_ps).then_inc(
                        S["full_done"], 1)
                b = at(-2)
                if b.live:
                    v.wait_ge(S["xn2T_mm"], b.n + 1)
                    wait(v, S["logit_mm"], b.n)
                    v.tensor_copy(xn2T[:, :], xn2T_ps).then_inc(S["xn2T_done"], 1)
                score(3, 0)
                b = at(4)
                if b.live:
                    v.wait_ge(S["relu_done"], b.n + 1)
                    wait(v, S["xn_done"], NT * b.n - NT)
                    for t in range(NT):
                        v.bn_stats(stats[b.par][:, t, :], tile_of(b, t)).then_inc(S["stat_dve"], 1)
                score(3, 1)
                if b.live:
                    v.wait_ge(S["stat_dve"], STAT * b.n + NT)
                    for t in range(NT):
                        v.bn_aggr(moments[b.par][:, t, :], stats[b.par][:, t, :]).then_inc(S["stat_dve"], 1)
                score(4, 0)
                route_logits(v, at(-2))
                score(4, 1)
                route_largest(v, at(-2))
                score(5, 0)
                route_index(v, at(-2))
                if b.live:
                    v.wait_ge(S["rstd_pool"], 2 * b.n + 2)
                    wait(v, S["xnT_mm"], b.n - 1)
                    for t in range(NT):
                        v.tensor_scalar(xn[b.par][:, t, :], tile_of(b, t), moments[b.par][:, t, 0:1],
                                        rstd[b.par][:, t:t + 1], ALU.subtract, ALU.mult).then_inc(S["xn_done"], 1)
                score(5, 1)
                route_choice(v, at(-2))
                b = at(-1)
                if b.live:
                    v.wait_ge(S["o_mm"], b.n + 1)
                    o = o_ps.rearrange("p (c w) -> p c w", w=VW)
                    wait(v, S["o_norm_done"], b.n)
                    v.reciprocal(o_rec[:, :].unsqueeze(2), o[:, :, HD:HD + 1]).then_inc(S["o_chain"], 1)
                route_mask(v, at(-2))
                score(6, 0)
                if b.live:
                    v.wait_ge(S["o_chain"], b.n + 1)
                    wait(v, S["hres_done"], b.n)
                    v.tensor_tensor(o_norm[:, :, :].rearrange("p t (h d) -> p (t h) d", d=HD), o[:, :, 0:HD],
                                    o_rec[:, :].unsqueeze(2).broadcast_to([P, NT * H, HD]), ALU.mult).then_inc(
                        S["o_norm_done"], 1)
                score(6, 1)
                if b.live:
                    v.wait_ge(S["o_norm_done"], b.n + 1)
                    h = hres[:, bass.ds(NT * b.n, NT), :]
                    v.tensor_tensor(h, h, o_norm[:, :, :], ALU.add).then_inc(S["hres_done"], 1)
                score(7, 0)
                if b.live:
                    v.wait_ge(S["hres_done"], b.n + 1)
                    wait(v, S["xn2_done"], NT * b.n)
                    for t in range(NT):
                        v.bn_stats(stats2[:, t, :], tile_of(b, t)).then_inc(S["ln2_dve"], 1)
                score(7, 1)
                if b.live:
                    v.wait_ge(S["ln2_dve"], LN2 * b.n + NT)
                    for t in range(NT):
                        v.bn_aggr(moments2[:, t, :], stats2[:, t, :]).then_inc(S["ln2_dve"], 1)
                    v.wait_ge(S["rstd2_pool"], RSTD2 * b.n + RSTD2)
                    wait(v, scattered[b.par], 16 * TOP_K * NT * b.half)
                    wait(v, S["xn2T_mm"], b.n - 1)
                    for t in range(NT):
                        v.tensor_scalar(xn2[b.par][:, t, :], tile_of(b, t), moments2[:, t, 0:1],
                                        rstd2[:, t:t + 1], ALU.subtract, ALU.mult).then_inc(S["xn2_done"], 1)

            run_steps(v, step)
            finish_vector(v)

        @block.tensor
        def _(pe):
            pe.wait_ge(S["const_pool"], POOL_CONSTANTS)
            pe.wait_ge(S["weights_in"], 80)
            for i in range(3):
                pe.transpose(bank_a[:, i * P:(i + 1) * P], w_nat[:, i, :], ident[:, :])
            pe.transpose(bank_a[:, 3 * P:3 * P + E], gate_nat[:, :], ident[0:E, 0:E])
            pe.transpose(bank_b[:, 0:VOCAB], emb_nat[:, :], ident[0:VOCAB, 0:VOCAB])
            pe.wait_ge(S["setup_dve"], CONTEXT)
            for k in range(CONTEXT):
                mm = pe.transpose(bank_b[:, (k + 1) * P:(k + 2) * P], conv_wide[:, k, :], ident[:, :])
            mm.then_inc(S["setup_pe"], 1)
            pe.wait_ge(S["setup_dve"], CONTEXT + 6)
            for k in range(CONTEXT):
                pe.matmul(bank_c[0:VOCAB, k * D:(k + 1) * D], embT[:, :], convT[:, k, :], start=True, stop=True)
            pe.matmul(bank_c[0:H, 2 * D:2 * D + NREL], bias_t[:, :], anti[0:NREL, 1:P], start=True,
                      stop=True).then_inc(S["setup_pe"], 1)
            pe.wait_ge(S["bias_wide"], 16)
            pe.wait_ge(S["bias_row"], 3)
            pe.wait_ge(S["table_done"], 1)
            for i in range(6):
                bank = (bank_a, bank_b, bank_c)[i % 3]
                if i >= 3:
                    pe.wait_ge(S["bias_done"], 3)
                h, u = divmod(i * 512, BIASW)
                at = 0
                while at < 512:
                    n = min(BIASW - u, 512 - at)
                    mm = pe.matmul(bank[:, at:at + n], anti[:, :], probs[:, h, u:u + n], start=True, stop=True)
                    at, u, h = at + n, 0, h + 1
                mm.then_inc(S["bias_ps"], 1)
            pe.wait_ge(S["bias_done"], 6)
            pe.wait_ge(S["const_dve"], DVE_CONSTANTS)

            def step(at):
                def score(h):
                    b = at(1)
                    if b.live:
                        if h == 0:
                            pe.wait_ge(stacked[b.par], 32 * len(TERMS) * b.half + 32 * len(TERMS))
                        wait(pe, S["scored_dve"], NT * (H * b.n + h - 1))
                        st = stack[b.par]
                        for t in range(NT):
                            mm = pe.matmul(ps_score[h % 2][:, t * T:(t + 1) * T], st[:, 0, h, t * P:(t + 1) * P],
                                           st[:, 1, h, :], start=True, stop=True)
                        mm.then_inc(S["scores_mm"], 1)

                def turn(b, h):
                    if not b.live:
                        return
                    wait(pe, S["exp_done"], H * b.n + h - 1)
                    pe.wait_ge(S["scored_dve"], NT * (H * b.n + h + 1))
                    bank = ps_turn[h % 2]
                    for j in range(NT):
                        for t in range(NT):
                            pe.matmul(bank[:, j * T + t * P:j * T + (t + 1) * P],
                                      scored[:, b.par, h, t * T + j * P:t * T + (j + 1) * P], ident[:, :],
                                      start=(j + t == 0), stop=False, is_transpose=True, skip_group_check=True)
                    if h == 0:
                        pe.wait_ge(S["maxT_done"], b.n + 1)
                    pe.matmul(bank[:, :].rearrange("p (j t) -> p j t", j=NT), minus_sel[:, h, :],
                              maxT[b.par][:, :].unsqueeze(1).broadcast_to([P, NT, T]),
                              start=False, stop=True, skip_group_check=True).then_inc(S["turned_mm"], 1)

                def values(b, group):
                    if not b.live:
                        return
                    pe.wait_ge(S["exp_done"], H * b.n + 4 * group + 4)
                    pe.wait_ge(S["v_done"], b.n + 1)
                    if group == 0:
                        wait(pe, S["oT_done"], b.n)
                    for j in range(NT):
                        for q in range(4):
                            h = 4 * group + q
                            mm = pe.matmul(ps_val[VW * q:VW * (q + 1), group * T:(group + 1) * T],
                                           v_op[b.quarter][:, j, h, :], probs[:, h, j * T:(j + 1) * T],
                                           start=(j == 0), stop=(j == NT - 1))
                    mm.then_inc(S["val_mm"], 1)

                score(0)
                turn(at(-1), 6)
                b = at(4)
                if b.live:
                    pe.wait_ge(S["onehot_done"], b.n + 1)
                    wait(pe, S["v_done"], b.n - 1)
                    wait(pe, S["w1_done"], b.n)
                    for t in range(NT):
                        for k in range(CONTEXT):
                            mm = pe.matmul(emb_ps[:, t * D:(t + 1) * D],
                                           onehot[b.par][0:VOCAB, t * P + k:t * P + k + P], table[0:VOCAB, k, :],
                                           start=(k == 0), stop=(k == CONTEXT - 1))
                    mm.then_inc(S["embed_mm"], 1)
                b = at(3)
                if b.live:
                    pe.wait_ge(S["xn_done"], NT * b.n + NT)
                    wait(pe, S["v_done"], b.n)
                    pe.wait_ge(S["w1_done"], b.n + 1)
                    for t in range(NT):
                        mm = pe.transpose(xnT_ps[:, t * P:(t + 1) * P], xn[b.par][:, t, :], ident[:, :])
                    mm.then_inc(S["xnT_mm"], 1)
                b = at(0)
                if b.live:
                    pe.wait_ge(S["max_split"], 2 * b.n + 2)
                    if at(-3).live:
                        wait(pe, S["slot_dve"], SLOT * at(-3).n + 1)
                    for t in range(NT):
                        mm = pe.transpose(max_ps[:, t * P:(t + 1) * P], max_parts[b.par][:, t, :], identb[:, :])
                    mm.then_inc(S["max_mm"], 1)
                score(1)
                turn(at(-1), 7)
                b = at(3)
                if b.live:
                    pe.wait_ge(S["xnT_done"], b.n + 1)
                    prev = at(-2)
                    if prev.live:
                        pe.wait_ge(S["o_norm_done"], prev.n + 1)
                    for side in range(2):
                        mm = pe.matmul(qk_ps[:, side * T:(side + 1) * T], wqkT[:, side, :], xnT[b.par][:, :],
                                       start=True, stop=True)
                    mm.then_inc(S["qk_mm"], 1)
                score(2)
                turn(at(0), 0)
                b = at(-2)
                if b.live:
                    pe.wait_ge(S["xn2_done"], NT * b.n + NT)
                    if at(0).live:
                        pe.wait_ge(S["maxT_done"], at(0).n + 1)
                    elif at(-3).live:
                        pe.wait_ge(S["slot_dve"], SLOT * at(-3).n + 1)
                    for t in range(NT):
                        mm = pe.transpose(xn2T_ps[:, t * P:(t + 1) * P], xn2[b.par][:, t, :], ident[:, :])
                    mm.then_inc(S["xn2T_mm"], 1)
                values(at(-1), 1)
                b = at(-2)
                if b.live:
                    pe.wait_ge(S["xn2T_done"], b.n + 1)
                    for t in range(NT):
                        mm = pe.matmul(logit_ps[:, t * E:(t + 1) * E], xn2T[:, t * P:(t + 1) * P], gateT[:, :],
                                       start=True, stop=True)
                    mm.then_inc(S["logit_mm"], 1)
                score(3)
                turn(at(0), 1)
                b = at(4)
                if b.live:
                    pe.wait_ge(w1_loaded[b.par], 16 * b.half + 16)
                    pe.wait_ge(S["relu_done"], b.n + 1)
                    prev = at(3)
                    if prev.live:
                        pe.wait_ge(S["xnT_done"], prev.n + 1)
                    for t in range(2):
                        mm = pe.transpose(w1_ps[:, t * P:(t + 1) * P], w1_in[b.par][:, t, :], ident[:, :])
                    mm.then_inc(S["w1_mm"], 1)
                score(4)
                turn(at(0), 2)
                b = at(-1)
                if b.live:
                    pe.wait_ge(S["oT_done"], b.n + 1)
                    other = at(3)
                    if other.live:
                        pe.wait_ge(S["part1_done"], other.n + 1)
                        pe.wait_ge(S["full_done"], other.n + 1)
                    for t in range(NT):
                        for group in range(2):
                            c = t * 2 + group
                            mm = pe.transpose(o_ps[:, c * P:(c + 1) * P],
                                              oT[:, group * T + t * P:group * T + (t + 1) * P], ident[:, :])
                    mm.then_inc(S["o_mm"], 1)
                score(5)
                turn(at(0), 3)
                b = at(3)
                if b.live:
                    other = at(4)
                    if other.live:
                        pe.wait_ge(S["w1_done"], other.n + 1)
                    for t in range(NT):
                        mm = pe.matmul(v_ps[:, t * D:(t + 1) * D], xnT[b.par][:, t * P:(t + 1) * P], wvT[:, :],
                                       start=True, stop=True)
                    mm.then_inc(S["v_mm"], 1)
                score(6)
                turn(at(0), 4)
                b = at(-2)
                if b.live:
                    pe.wait_ge(S["route_dve"], ROUTE * b.n + ROUTE)
                    pe.wait_ge(S["count_pool"], COUNT * b.n + 1)
                    for t in range(NT):
                        pe.matmul(rank_ps[:, t * E:(t + 1) * E], earlier[:, :], mask[b.par][:, t, :],
                                  start=True, stop=False)
                        mm = pe.matmul(rank_ps[:, t * E:(t + 1) * E], onesb[:, :], before[b.par][:, t, :],
                                       start=False, stop=True)
                    mm.then_inc(S["rank_mm"], 1)
                score(7)
                turn(at(0), 5)
                values(at(0), 0)

            run_steps(pe, step)
            finish_tensor(pe)


_INS = ["x", "L0_tok_emb_table", "L0_tok_conv_w", "L0_attn_Wq", "L0_attn_Wk", "L0_attn_Wv", "L0_attn_rel_pos_bias",
        "L0_ffn_gate_weight", "L0_ffn_w1", "L0_ffn_w2"]


def kernel(**inputs):
    import numpy as _np
    import concourse.bacc as _bacc
    from concourse import mybir as _mybir
    from concourse.bass_utils import run_bass_kernel_spmd as _run

    nc = _bacc.Bacc("TRN2", target_bir_lowering=False, num_devices=1)
    arrays, args = {}, []
    for name in _INS:
        a = _np.ascontiguousarray(inputs[name])
        arrays[f"in_{name}"] = a
        args.append(nc.dram_tensor(f"in_{name}", a.shape, _mybir.dt.from_np(a.dtype), kind="ExternalInput").ap())
    out = nc.dram_tensor("out_0", (BATCH, T, D), _mybir.dt.float32, kind="ExternalOutput").ap()
    tower_kernel(nc, *args, out)
    r = _run(nc, [arrays], core_ids=[0])
    return r.results[0]["out_0"]
```

```python
from contextlib import ExitStack

import concourse.bass as bass
from concourse import mybir

F32 = mybir.dt.float32
BF16 = mybir.dt.bfloat16
I32 = mybir.dt.int32
U32 = mybir.dt.uint32
ALU = mybir.AluOpType
ACT = mybir.ActivationFunctionType
AX = mybir.AxisListType

P = 128
BATCH, T, D = 32, 256, 128
NT = T // P
TILES = BATCH * NT
H, HD = 8, 16
VW = 32
VOCAB, CONTEXT, GROUP = 125, 2, 4
WINDOW = 64
NREL = 2 * WINDOW - 1
BIASW = NT * P + P
E, F = 16, 512
TOP_K = 2
CAP = BATCH * T + P
ZERO_ROW = E * CAP
BLOCKS = -(-(BATCH * T * TOP_K // P + E - 1) // 8) * 8
ZERO_PARTS = 16
UNROLL = 8
AHEAD = 2
EPS = 1e-5
TURNS = BLOCKS // UNROLL
assert TURNS - 2 == E
LOW = -3.0e38
TERMS = [(0, 0), (0, 1), (1, 0), (1, 1), (0, 2), (2, 0)]
KROWS = len(TERMS) * HD
POOL_CONSTANTS, DVE_CONSTANTS = 23, 16
IDENT_MADE, GROUPS_MADE = 7, 9
FIRST_STEP, LAST_STEP = -5, BATCH + 2
BIAS_STEP = -2


class Batch:
    def __init__(self, n):
        self.n = n
        self.par = n % 2
        self.quarter = n % 4
        self.half = n // 2
        self.live = 0 <= n < BATCH


def run_steps(eng, step):
    for s in range(FIRST_STEP, LAST_STEP + 1):
        step(lambda d: Batch(s + d))


def run_turns(eng, turn):
    turn(0)
    with eng.Fori(1, TURNS - 1) as i:
        turn(i)
    turn(TURNS - 1)


def wait(eng, semaphore, count):
    if not isinstance(count, int) or count > 0:
        eng.wait_ge(semaphore, count)


def tower_kernel(nc, x, emb, conv_w, wq, wk, wv, rel_bias, gate_w, w1, w2, out):
    with ExitStack() as ctx:
        def sb(name, shape, dt=F32):
            return ctx.enter_context(nc.sbuf_tensor(name, shape, dt))

        def pb(name, shape=(P, 512), dt=F32):
            return ctx.enter_context(nc.psum_tensor(name, list(shape), dt))

        def sem(name):
            return ctx.enter_context(nc.semaphore(name))

        expert_rows = nc.dram_tensor("expert_rows", (ZERO_ROW + P, D), F32)
        bias_rows = nc.dram_tensor("bias_rows", (H, 512), F32)

        ident = sb("ident", [P, P])
        identb = sb("identb", [P, P], BF16)
        anti = sb("anti", [P, P])
        onesf = sb("onesf", [P, P])
        onesb = sb("onesb", [P, P], BF16)
        earlier = sb("earlier", [P, P], BF16)
        minus_sel = sb("minus_sel", [P, H, P], BF16)
        group_mask = sb("group_mask", [P, P])
        tile_mask = sb("tile_mask", [P, 8])
        vocab_i = sb("vocab_i", [P, 1], I32)
        vocab_f = sb("vocab_f", [P, 1])
        expert_i = sb("expert_i", [P, E], I32)
        expert_f = sb("expert_f", [P, E])
        region = sb("region", [P, E])
        minus_half = sb("minus_half", [P, NT])
        zeros = sb("zeros", [P, P])
        w_nat = sb("w_nat", [P, 3, P])
        gate_nat = sb("gate_nat", [E, D])
        emb_nat = sb("emb_nat", [VOCAB, D])
        conv_nat = sb("conv_nat", [P, GROUP, CONTEXT])
        bias_t = sb("bias_t", [NREL, H])
        conv_wide = sb("conv_wide", [P, CONTEXT, P])
        wqkT = sb("wqkT", [P, 2, P])
        wvT = sb("wvT", [P, P])
        gateT = sb("gateT", [P, E])
        embT = sb("embT", [P, VOCAB])
        convT = sb("convT", [P, CONTEXT, P])
        table = sb("table", [P, CONTEXT, D])
        bias_ext = sb("bias_ext", [H, 512])
        arena = sb("arena", [P, E * F])
        stack_cols = 2 * H * T // 2
        stack = [arena[0:KROWS, i * stack_cols:(i + 1) * stack_cols].bitcast(BF16).rearrange(
            "p (s h t) -> p s h t", s=2, h=H) for i in range(2)]
        bias_at, rest_at = 2 * stack_cols, 2 * stack_cols + H * BIASW
        bias_flat = arena[:, bias_at:rest_at]
        bias = bias_flat.rearrange("p (h u) -> p h u", h=H)
        qk_rest = [arena[:, rest_at + i * 2 * T:rest_at + (i + 1) * 2 * T].rearrange(
            "p (s t) -> p s t", s=2) for i in range(2)]
        w2_nat = arena[:, :].rearrange("p (e f) -> p e f", e=E)
        w1_in = [sb(f"w1_in{i}", [P, 2, D]) for i in range(2)]
        w1T = sb("w1T", [P, E * F])
        tok = [sb(f"tok{i}", [P, T], I32) for i in range(2)]
        onehot = [sb(f"onehot{i}", [P, 1 + T]) for i in range(2)]
        hres = sb("hres", [P, TILES, D])
        stats = [sb(f"stats{i}", [P, NT, 6]) for i in range(2)]
        moments = [sb(f"moments{i}", [P, NT, 2]) for i in range(2)]
        var_eps = [sb(f"var_eps{i}", [P, NT]) for i in range(2)]
        rstd = [sb(f"rstd{i}", [P, NT]) for i in range(2)]
        xn = [sb(f"xn{i}", [P, NT, D]) for i in range(2)]
        xnT = [sb(f"xnT{i}", [P, T]) for i in range(2)]
        qk_part = [sb(f"qk_part{i}", [P, 2, 3, T], BF16) for i in range(2)]
        v_op = [sb(f"v_op{i}", [P, NT, H, VW]) for i in range(4)]
        scored = sb("scored", [P, 2, H, NT * T])
        row_max = [sb(f"row_max{i}", [P, NT, H]) for i in range(2)]
        max_parts = [sb(f"max_parts{i}", [P, NT, 2 * H], BF16) for i in range(2)]
        maxT = [sb(f"maxT{i}", [P, T], BF16) for i in range(2)]
        probs = sb("probs", [P, H, NT * T])
        oT = sb("oT", [P, 2 * T])
        o_rec = sb("o_rec", [P, NT * H])
        o_norm = sb("o_norm", [P, NT, D])
        stats2 = sb("stats2", [P, NT, 6])
        moments2 = sb("moments2", [P, NT, 2])
        var_eps2 = sb("var_eps2", [P, NT])
        rstd2 = sb("rstd2", [P, NT])
        xn2 = [sb(f"xn2_{i}", [P, NT, D]) for i in range(2)]
        xn2T = sb("xn2T", [P, T])
        logits = sb("logits", [P, NT, E])
        largest = sb("largest", [P, NT, 8])
        largest_at = sb("largest_at", [P, NT, 8], U32)
        chosen = [sb(f"chosen{i}", [P, TOP_K, NT, E]) for i in range(2)]
        mask = [sb(f"mask{i}", [P, NT, E], BF16) for i in range(2)]
        before = [sb(f"before{i}", [P, NT, E], BF16) for i in range(2)]
        slot = sb("slot", [P, NT, E])
        slot_of = sb("slot_of", [P, TOP_K, NT, E])
        slot_f = sb("slot_f", [P, TOP_K * NT])
        slot_i = [sb(f"slot_i{i}", [P, TOP_K * NT], I32) for i in range(2)]
        gap_all = sb("gap_all", [P, TILES])
        chosen_all = sb("chosen_all", [P, TOP_K, TILES, E], BF16)

        sums = scored[:, :, :, :].rearrange("p a h t -> p (a h t)")
        hidden = [probs[:, i, :] for i in range(2)]
        block_rows = [probs[:, 2, i * D:(i + 1) * D] for i in range(4)] + [
            xnT[i // 2][:, (i % 2) * D:(i % 2 + 1) * D] for i in range(4)]
        y_prod = [probs[:, 6 + i, :] for i in range(2)]
        blockT = [probs[:, 5, i * P:(i + 1) * P] for i in range(4)]
        counts = sb("counts", [P, E])
        counts1 = sb("counts1", [P, E])
        per_token = sb("per_token", [P, E])
        end_i = sb("end_i", [P, E], I32)
        blocks_i = sb("blocks_i", [P, E], I32)
        blocks_s = sb("blocks_s", [P, E], I32)
        blocks = sb("blocks", [P, E])
        block_end = sb("block_end", [P, E])
        block_k = sb("block_k", [P, 2])
        passed = w_nat[:, 1, 0:2 * E].rearrange("p (c e) -> p c e", c=2)
        passed_blocks = w_nat[:, 1, 2 * E:4 * E].rearrange("p (c e) -> p c e", c=2)
        plan_e = sb("plan_e", [P, 2])
        plan_b = sb("plan_b", [P, 2])
        plan_l = sb("plan_l", [P, 2])
        plan_f = sb("plan_f", [P, 4])
        plan_i = sb("plan_i", [1, 4 * P], I32)
        gap_exp = sb("gap_exp", [P, TILES])
        gap_exp1 = sb("gap_exp1", [P, TILES])
        share = sb("share", [P, TOP_K, TILES])
        gates_k = arena[:, E * F - TOP_K * TILES * E:E * F].rearrange("p (k t e) -> p k t e", k=TOP_K, e=E)
        gates = sb("gates", [P, TILES, E])
        gateT_all = probs[:, 3:5, :].rearrange("p a (g t) -> p (a g) t", t=P)
        yT = sb("yT", [P, E])
        y_wide = w_nat[:, 0, :].rearrange("p (a e) -> p a e", a=8)
        y_block = gates[:, :, :].rearrange("p (t a) e -> p t (a e)", t=8)

        ps_score = [pb(f"ps_score{i}") for i in range(2)]
        ps_turn = [pb(f"ps_turn{i}") for i in range(2)]
        ps_val = pb("ps_val")
        bank_a, bank_b, bank_c = pb("bank_a"), pb("bank_b"), pb("bank_c")
        emb_ps, xnT_ps = bank_a[:, 0:T], bank_a[:, T:2 * T]
        v_ps, w1_ps = bank_a[:, 0:T], bank_a[:, T:2 * T]
        qk_ps = bank_b[:, :]
        o_ps = bank_b[:, :]
        xn2T_ps = bank_c[:, 0:T]
        max_ps = bank_c[0:2 * H, T:T + P].bitcast(BF16)
        logit_ps = bank_c[:, 384:384 + NT * E]
        rank_ps = bank_c[:, 416:416 + NT * E]

        bias_banks = ps_score + ps_turn + [ps_val, bank_c]
        up_ps = ps_score + ps_turn
        turn_ps = [bank[:, 0:P] for bank in (bank_a, bank_b, bank_c, ps_val)]

        names = """plan_done padded block_turned result_done stored sums_zero gap_exp_done gate_mm gateT_done up_mm
        summed silu_done plan_dve plan_ready plan_mm count_mm gates_done blockT_done spread_mm y_done y_wide_done y_mm
        y_block_done mix_mm weights_in conv_in bias_t_in bias_in bias_row bias_wide const_pool const_dve setup_pe setup_dve table_done block_k_done
        bias_ps bias_done w2_in zero_row_out onehot_done embed_mm relu_done stat_dve rstd_pool xn_done xnT_mm xnT_done
        w1_mm w1_done qk_mm part1_done rest_done split_pool part2_done v_mm v_done scores_mm scored_dve
        max_split max_mm maxT_done turned_mm exp_done val_mm oT_done o_mm o_chain o_norm_done hres_done
        ln2_dve rstd2_pool xn2_done xn2T_mm xn2T_done logit_mm route_dve gap_done chosen_kept count_dve rank_mm slot_dve""".split()
        S = {n: sem(n) for n in names}
        tok_in = [sem(f"tok_in{i}") for i in range(2)]
        w1_loaded = [sem(f"w1_loaded{i}") for i in range(2)]
        scattered = [sem(f"scattered{i}") for i in range(2)]
        block_in = [sem(f"block_in{i}") for i in range(UNROLL)]
        stacked = [sem(f"stacked{i}") for i in range(2)]
        STAT, LN2, RSTD2, ROUTE, COUNT, SLOT = 4, 4, 2, 8, 2, 4

        SP, PE, DVE = mybir.EngineType.SP, mybir.EngineType.PE, mybir.EngineType.DVE

        def plan_values(engine, at, largest_value):
            values = []
            for half in range(UNROLL // 4):
                _, four = nc.values_load_multi_w_load_instructions(
                    plan_i[0:1, bass.ds(at + 4 * half, 4)], engines=[engine], min_val=0, max_val=largest_value,
                    skip_runtime_bounds_check_because="the plan is made on the chip from counts and cut to this range")
                values += list(four)
            return values

        def zero_ends(eng, engine, half):
            for quad in range(2):
                first = E // 2 * half + 4 * quad
                _, ends = nc.values_load_multi_w_load_instructions(
                    end_i[0:1, first:first + 4], engines=[engine], min_val=0, max_val=ZERO_ROW - P,
                    skip_runtime_bounds_check_because="a region's start and a count of at most every token")
                for end in ends:
                    eng.dma_start(expert_rows[bass.ds(end, P), :], zeros[:, :]).then_inc(S["padded"], 16)

        def zero_sums(eng, first, last):
            eng.wait_ge(S["turned_mm"], H * BATCH)
            for i in range(first, last):
                part = sums[:, i * (E * F // ZERO_PARTS):(i + 1) * (E * F // ZERO_PARTS)]
                if eng is nc.vector:
                    ins = eng.memset(part, 0.0)
                else:
                    ins = eng.copy(part.rearrange("p (a b) -> p a b", b=P),
                                   zeros[:, :].unsqueeze(1).broadcast_to([P, E * F // ZERO_PARTS // P, P]))
                ins.then_inc(S["sums_zero"], 1)

        def route_logits(v, b):
            if b.live:
                v.wait_ge(S["logit_mm"], b.n + 1)
                v.tensor_copy(logits[:, :, :].rearrange("p t e -> p (t e)"), logit_ps).then_inc(S["route_dve"], 1)

        def route_largest(v, b):
            if b.live:
                v.wait_ge(S["route_dve"], ROUTE * b.n + 1)
                for t in range(NT):
                    v.max(largest[:, t, :], logits[:, t, :]).then_inc(S["route_dve"], 1)

        def route_index(v, b):
            if b.live:
                v.wait_ge(S["route_dve"], ROUTE * b.n + 1 + NT)
                for t in range(NT):
                    v.max_index(largest_at[:, t, :], largest[:, t, :], logits[:, t, :]).then_inc(S["route_dve"], 1)

        def route_choice(v, b):
            if b.live:
                v.wait_ge(S["route_dve"], ROUTE * b.n + 1 + 2 * NT)
                wait(v, S["chosen_kept"], b.n - 1)
                wait(v, S["slot_dve"], SLOT * b.n - SLOT)
                for k in range(TOP_K):
                    at = largest_at[:, :, k:k + 1].broadcast_to([P, NT, E])
                    ex = expert_f[:, :].unsqueeze(1).broadcast_to([P, NT, E])
                    v.tensor_tensor(chosen[b.par][:, k, :, :], ex, at, ALU.is_equal).then_inc(S["route_dve"], 1)
                v.tensor_tensor(gap_all[:, bass.ds(NT * b.n, NT)].unsqueeze(2), largest[:, :, 1:2],
                                largest[:, :, 0:1], ALU.subtract).then_inc(S["gap_done"], 1)

        def route_mask(v, b):
            if b.live:
                v.wait_ge(S["route_dve"], ROUTE * b.n + 1 + 2 * NT + TOP_K)
                v.wait_ge(S["gap_done"], b.n + 1)
                wait(v, S["rank_mm"], b.n - 1)
                wait(v, S["count_dve"], COUNT * b.n - COUNT)
                v.tensor_tensor(mask[b.par][:, :, :], chosen[b.par][:, 0, :, :], chosen[b.par][:, 1, :, :],
                                ALU.add).then_inc(S["route_dve"], 1)

        def route_count(v, b, tile):
            if b.live:
                cur, nxt, m = before[b.par], before[1 - b.par], mask[b.par]
                if tile == 0:
                    v.wait_ge(S["route_dve"], ROUTE * b.n + ROUTE)
                    wait(v, S["count_dve"], COUNT * b.n)
                    v.tensor_tensor(cur[:, 1, :], cur[:, 0, :], m[:, 0, :], ALU.add).then_inc(S["count_dve"], 1)
                else:
                    v.wait_ge(S["count_dve"], COUNT * b.n + 1)
                    wait(v, S["rank_mm"], b.n)
                    v.tensor_tensor(nxt[:, 0, :], cur[:, 1, :], m[:, 1, :], ALU.add).then_inc(S["count_dve"], 1)

        def place(v, b, stage):
            if not b.live:
                return
            if stage == 0:
                v.wait_ge(S["rank_mm"], b.n + 1)
                wait(v, S["slot_dve"], SLOT * b.n)
                v.tensor_tensor(slot[:, :, :], rank_ps.rearrange("p (t e) -> p t e", e=E),
                                region[:, :].unsqueeze(1).broadcast_to([P, NT, E]), ALU.add).then_inc(
                    S["slot_dve"], 1)
            if stage == 1:
                v.wait_ge(S["slot_dve"], SLOT * b.n + 1)
                v.tensor_tensor(slot_of[:, :, :, :], chosen[b.par][:, :, :, :],
                                slot[:, :, :].unsqueeze(1).broadcast_to([P, TOP_K, NT, E]), ALU.mult).then_inc(
                    S["slot_dve"], 1)
            if stage == 2:
                v.wait_ge(S["slot_dve"], SLOT * b.n + 2)
                v.tensor_reduce(slot_f[:, :], slot_of[:, :, :, :].rearrange("p k t e -> p (k t) e"), AX.X,
                                ALU.add).then_inc(S["slot_dve"], 1)
            if stage == 3:
                v.wait_ge(S["slot_dve"], SLOT * b.n + 3)
                wait(v, scattered[b.par], 16 * TOP_K * NT * b.half)
                v.tensor_copy(slot_i[b.par][:, :], slot_f[:, :]).then_inc(S["slot_dve"], 1)

        def finish_sync(sp):
            sp.wait_ge(S["plan_done"], 1)
            zero_ends(sp, mybir.EngineType.SP, 0)
            sp.wait_ge(S["zero_row_out"], 16)
            sp.wait_ge(S["padded"], 16 * E)
            for i in range(2):
                sp.wait_ge(scattered[i], 16 * TOP_K * TILES // 2)
            sp.wait_ge(S["val_mm"], 2 * BATCH)
            sp.wait_ge(S["plan_done"], 2)

            def load(turn):
                if not isinstance(turn, int):
                    sp.wait_ge(S["gates_done"], 1)
                    sp.dma_start(w2_nat[:, bass.ds(turn + -1, 1), :],
                                 w2[bass.ds(turn + -1, 1), :, :].rearrange("e d f -> d e f")).then_inc(S["w2_in"], 16)
                rows = plan_values(SP, UNROLL * turn, ZERO_ROW)
                for u, row in enumerate(rows):
                    wait(sp, S["block_turned"], UNROLL * turn + u - UNROLL + 1)
                    sp.dma_start(block_rows[u], expert_rows[bass.ds(row, P), :]).then_inc(block_in[u], 16)

            run_turns(sp, load)
            out_v = out.rearrange("b (t p) d -> p (b t) d", p=P)
            for i in range(TILES // 4):
                sp.wait_ge(S["result_done"], i + 1)
                sp.dma_start(out_v[:, 4 * i:4 * i + 4, :], hres[:, 4 * i:4 * i + 4, :]).then_inc(S["stored"], 16)
            sp.wait_ge(S["stored"], 16 * (TILES // 4))

        def finish_scalar(act):
            act.wait_ge(S["gap_done"], BATCH)
            act.activation(gap_exp[:, :], gap_all[:, :], ACT.Exp).then_inc(S["gap_exp_done"], 1)
            act.wait_ge(S["plan_done"], 1)
            zero_ends(act, mybir.EngineType.Activation, 1)
            def copy_rows(k, u):
                act.wait_ge(S["block_turned"], k + 1)
                act.copy(blockT[u % 4], turn_ps[u % 4]).then_inc(S["blockT_done"], 1)

            def silu(k, u):
                act.wait_ge(S["up_mm"], k + 1)
                wait(act, S["summed"], k - 1)
                act.activation(hidden[u % 2], up_ps[u % 4][:, :], ACT.Silu).then_inc(S["silu_done"], 1)

            for u in range(AHEAD):
                copy_rows(u, u)

            def turn_of_blocks(turn):
                for u in range(UNROLL):
                    if not isinstance(turn, int) or turn < TURNS - 1 or u < UNROLL - AHEAD:
                        copy_rows(UNROLL * turn + u + AHEAD, u + AHEAD)
                    silu(UNROLL * turn + u, u)

            run_turns(act, turn_of_blocks)
            for i, bank in enumerate((bank_a, bank_b)):
                act.wait_ge(S["gate_mm"], i + 1)
                act.copy(gateT_all[:, 4 * i:4 * i + 4, :].rearrange("p g t -> p (g t)"), bank[:, :]).then_inc(
                    S["gateT_done"], 1)

        def finish_vector(v):
            done = 0

            def link(ins):
                nonlocal done
                done += 1
                ins.then_inc(S["plan_dve"], 1)
                v.wait_ge(S["plan_dve"], done)

            v.wait_ge(S["count_mm"], 1)
            link(v.tensor_copy(counts[:, :], bank_c[:, 0:E]))
            v.tensor_tensor(end_i[:, :], counts[:, :], region[:, :], ALU.add).then_inc(S["plan_done"], 1)
            link(v.tensor_scalar(blocks_i[:, :], counts[:, :], float(P - 1), None, ALU.add))
            link(v.tensor_single_scalar(blocks_s[:, :], blocks_i[:, :], 7, ALU.arith_shift_right))
            link(v.tensor_copy(blocks[:, :], blocks_s[:, :]))
            link(v.tensor_tensor_scan(block_end[:, :], onesf[:, 0:E], blocks[:, :], 0.0, ALU.mult, ALU.add))
            wide = [P, 2, E]
            v.wait_ge(S["block_k_done"], 2)
            link(v.tensor_tensor(passed[:, :, :], block_end[:, :].unsqueeze(1).broadcast_to(wide),
                                 block_k[:, :].unsqueeze(2).broadcast_to(wide), ALU.is_le))
            link(v.tensor_reduce(plan_e[:, :], passed[:, :, :], AX.X, ALU.add))
            link(v.tensor_tensor(passed_blocks[:, :, :], passed[:, :, :],
                                 blocks[:, :].unsqueeze(1).broadcast_to(wide), ALU.mult))
            link(v.tensor_reduce(plan_b[:, :], passed_blocks[:, :, :], AX.X, ALU.add))
            link(v.tensor_tensor(plan_b[:, :], block_k[:, :], plan_b[:, :], ALU.subtract))
            link(v.tensor_scalar(plan_l[:, :], plan_e[:, :], float(E), float(P), ALU.is_lt, ALU.mult))
            link(v.tensor_tensor(plan_b[:, :], plan_b[:, :], plan_l[:, :], ALU.mult))
            link(v.scalar_tensor_tensor(out=plan_f[:, 0:2], in0=plan_e[:, :], scalar=float(CAP),
                                        in1=plan_b[:, :], op0=ALU.mult, op1=ALU.add))
            link(v.tensor_scalar(plan_f[:, 2:4], plan_e[:, :], float(E - 1), float(F), ALU.min, ALU.mult))
            v.sem_inc(S["plan_ready"], 1)
            v.wait_ge(S["plan_mm"], 1)
            v.tensor_copy(plan_i[:, :], bank_c[0:1, :]).then_inc(S["plan_done"], 1)
            v.wait_ge(S["gap_exp_done"], 1)
            v.wait_ge(S["chosen_kept"], BATCH)
            v.wait_ge(S["val_mm"], 2 * BATCH)
            link(v.tensor_scalar(gap_exp1[:, :], gap_exp[:, :], 1.0, None, ALU.add))
            link(v.reciprocal(share[:, 0, :], gap_exp1[:, :]))
            link(v.tensor_tensor(share[:, 1, :], gap_exp[:, :], share[:, 0, :], ALU.mult))
            for k in range(TOP_K):
                link(v.tensor_tensor(gates_k[:, k, :, :], chosen_all[:, k, :, :],
                                     share[:, k, :].unsqueeze(2).broadcast_to([P, TILES, E]), ALU.mult))
            v.tensor_tensor(gates[:, :, :], gates_k[:, 0, :, :], gates_k[:, 1, :, :], ALU.add).then_inc(
                S["gates_done"], 1)

            v.wait_ge(S["plan_done"], 2)
            v.wait_ge(S["sums_zero"], ZERO_PARTS)

            def add_hidden(turn):
                places = plan_values(DVE, 2 * P + UNROLL * turn, (E - 1) * F)
                for u, at in enumerate(places):
                    v.wait_ge(S["silu_done"], UNROLL * turn + u + 1)
                    wait(v, S["summed"], UNROLL * turn + u)
                    here = sums[:, bass.ds(at, F)]
                    v.tensor_tensor(here, here, hidden[u % 2], ALU.add).then_inc(S["summed"], 1)

            run_turns(v, add_hidden)
            v.wait_ge(S["w2_in"], 16 * E)
            for e in range(E):
                v.wait_ge(S["spread_mm"], e + 1)
                wait(v, S["y_done"], e - 1)
                v.tensor_tensor_reduce(y_prod[e % 2], up_ps[e % 4][:, :], w2_nat[:, e, :], 1.0, 0.0, ALU.mult,
                                       ALU.add, yT[:, e:e + 1]).then_inc(S["y_done"], 1)
            v.wait_ge(S["y_done"], E)
            link(v.tensor_scalar(counts1[:, :], counts[:, :], 1.0, None, ALU.max))
            link(v.reciprocal(per_token[:, :], counts1[:, :]))
            v.tensor_tensor(y_wide[:, :, :], yT[:, :].unsqueeze(1).broadcast_to([P, 8, E]),
                            per_token[:, :].unsqueeze(1).broadcast_to([P, 8, E]), ALU.mult).then_inc(S["y_wide_done"], 1)
            v.wait_ge(S["y_mm"], 1)
            v.tensor_tensor(y_block[:, :, :], bank_c[:, 0:P].unsqueeze(1).broadcast_to([P, 8, D]),
                            tile_mask[:, :].unsqueeze(2).broadcast_to([P, 8, D]), ALU.mult).then_inc(
                S["y_block_done"], 1)
            for i in range(TILES // 4):
                v.wait_ge(S["mix_mm"], i + 1)
                here = hres[:, 4 * i:4 * i + 4, :].rearrange("p t d -> p (t d)")
                v.tensor_tensor(here, here, up_ps[i % 4][:, :], ALU.add).then_inc(S["result_done"], 1)

        def finish_tensor(pe):
            pe.wait_ge(S["count_dve"], COUNT * BATCH)
            pe.wait_ge(S["slot_dve"], SLOT * BATCH)
            pe.matmul(bank_c[:, 0:E], onesb[:, :], before[BATCH % 2][:, 0, :], start=True, stop=True).then_inc(
                S["count_mm"], 1)
            pe.wait_ge(S["plan_ready"], 1)
            for c in range(4):
                mm = pe.transpose(bank_c[0:1, c * P:(c + 1) * P], plan_f[:, c:c + 1], ident[:, :])
            mm.then_inc(S["plan_mm"], 1)
            pe.wait_ge(S["v_done"], BATCH)
            pe.wait_ge(S["w1_done"], BATCH)
            pe.wait_ge(S["o_norm_done"], BATCH)
            pe.wait_ge(S["oT_done"], BATCH)
            pe.wait_ge(S["plan_done"], 2)
            pe.wait_ge(S["exp_done"], H * BATCH)

            def turn_rows(turn, u):
                pe.wait_ge(block_in[u], 16 * turn + 16)
                pe.transpose(turn_ps[u % 4], block_rows[u], ident[:, :]).then_inc(S["block_turned"], 1)

            def products(turn):
                for u, at in enumerate(plan_values(PE, 2 * P + UNROLL * turn, (E - 1) * F)):
                    k = UNROLL * turn + u
                    if u < UNROLL - AHEAD:
                        turn_rows(turn, u + AHEAD)
                    elif not isinstance(turn, int) or turn < TURNS - 1:
                        turn_rows(turn + 1, u + AHEAD - UNROLL)
                    pe.wait_ge(S["blockT_done"], k + 1)
                    wait(pe, S["silu_done"], k - 3)
                    pe.matmul(up_ps[u % 4][:, :], blockT[u % 4], w1T[:, bass.ds(at, F)], start=True,
                              stop=True).then_inc(S["up_mm"], 1)

            for u in range(AHEAD):
                turn_rows(0, u)
            run_turns(pe, products)
            pe.wait_ge(S["gates_done"], 1)
            for g in range(8):
                mm = pe.transpose((bank_a, bank_b)[g // 4][:, (g % 4) * P:(g % 4 + 1) * P],
                                  gates[:, 8 * g:8 * g + 8, :].rearrange("p t e -> p (t e)"), ident[:, :])
                if g % 4 == 3:
                    mm.then_inc(S["gate_mm"], 1)
            pe.wait_ge(S["summed"], BLOCKS)
            for e in range(E):
                wait(pe, S["y_done"], e - 3)
                pe.matmul(up_ps[e % 4][:, :], onesf[:, :], sums[:, e * F:(e + 1) * F], start=True,
                          stop=True).then_inc(S["spread_mm"], 1)
            pe.wait_ge(S["y_wide_done"], 1)
            pe.transpose(bank_c[:, 0:P], y_wide[:, :, :].rearrange("p t e -> p (t e)"), ident[:, :]).then_inc(
                S["y_mm"], 1)
            pe.wait_ge(S["y_block_done"], 1)
            pe.wait_ge(S["gateT_done"], 2)
            for i in range(TILES // 4):
                wait(pe, S["result_done"], i - 3)
                pe.matmul(up_ps[i % 4][:, :], gateT_all[:, i // 2, :],
                          y_block[:, 4 * (i % 2):4 * (i % 2) + 4, :].rearrange("p t d -> p (t d)"), start=True,
                          stop=True).then_inc(S["mix_mm"], 1)

        block = ctx.enter_context(nc.Block())

        @block.sync
        def _(sp):
            sp.dma_start(w_nat[:, 0, :], wq).then_inc(S["weights_in"], 16)
            sp.dma_start(w_nat[:, 1, :], wk).then_inc(S["weights_in"], 16)
            sp.dma_start(w_nat[:, 2, :], wv).then_inc(S["weights_in"], 16)
            sp.dma_start(gate_nat[:, :], gate_w).then_inc(S["weights_in"], 16)
            sp.dma_start(emb_nat[:, :], emb).then_inc(S["weights_in"], 16)

            def shift_bias():
                sp.wait_ge(S["bias_row"], 3)
                sp.dma_start(bias_rows[:, :], bias_ext[:, :]).then_inc(S["bias_in"], 16)
                sp.wait_ge(S["bias_in"], 16)
                shifted = bass.AP(bias_rows, 0, [[1, P], [512, H], [1, BIASW]])
                sp.dma_start(probs[:, :, 0:BIASW], shifted).then_inc(S["bias_wide"], 16)

            def step(at):
                if at(0).n == BIAS_STEP - 1:
                    shift_bias()
                b = at(5)
                if b.live:
                    wait(sp, S["onehot_done"], b.n - 1)
                    row = x[bass.ds(b.n, 1), :]
                    sp.dma_start(tok[b.par][:, :], row.partition_broadcast(P)).then_inc(tok_in[b.par], 16)
                    wait(sp, S["w1_mm"], b.n - 1)
                    rows = w1.rearrange("e f d -> (e f) d")[bass.ds(b.n * 2 * P, 2 * P), :]
                    sp.dma_start(w1_in[b.par][:, :, :], rows.rearrange("(t p) d -> p t d", p=P)).then_inc(
                        w1_loaded[b.par], 16)
                b = at(3)
                if b.live:
                    sp.wait_ge(S["split_pool"], b.n + 1)
                    sp.wait_ge(S["part2_done"], b.n + 1)
                    wait(sp, S["scores_mm"], H * b.n - H)
                    for i, (pq, pk) in enumerate(TERMS):
                        for side, part in ((0, pq), (1, pk)):
                            sp.dma_start(stack[b.par][i * HD:(i + 1) * HD, side, :, :],
                                         qk_part[b.par][:, side, part, :]).then_inc(stacked[b.par], 16)

            run_steps(sp, step)
            finish_sync(sp)

        @block.gpsimd
        def _(g):
            done = 0

            def tick(ins):
                nonlocal done
                done += 1
                ins.then_inc(S["const_pool"], 1)

            def made():
                g.wait_ge(S["const_pool"], done)

            tick(g.memset(ident[:, :], 0.0))
            tick(g.memset(identb[:, :], 0.0))
            tick(g.memset(anti[:, :], 0.0))
            tick(g.memset(group_mask[:, :], 1.0))
            made()
            diag = dict(compare_op=ALU.not_equal, fill=1.0, base=0, pattern=[[-1, P]], channel_multiplier=1)
            tick(g.affine_select(out=ident[:, :], in_=ident[:, :], **diag))
            tick(g.affine_select(out=identb[:, :], in_=identb[:, :], **diag))
            tick(g.affine_select(out=anti[:, :], in_=anti[:, :], compare_op=ALU.not_equal, fill=1.0,
                                 base=-(P - 1), pattern=[[1, P]], channel_multiplier=1))
            tick(g.affine_select(out=group_mask[:, :], in_=group_mask[:, :], compare_op=ALU.is_ge, fill=0.0,
                                 base=0, pattern=[[-GROUP, P // GROUP], [0, GROUP]], channel_multiplier=1))
            made()
            tick(g.affine_select(out=group_mask[:, :], in_=group_mask[:, :], compare_op=ALU.is_ge, fill=0.0,
                                 base=GROUP - 1, pattern=[[GROUP, P // GROUP], [0, GROUP]], channel_multiplier=-1))
            tick(g.iota(vocab_i[:, :], pattern=[[0, 1]], base=0, channel_multiplier=1))
            tick(g.iota(expert_i[:, :], pattern=[[1, E]], base=0, channel_multiplier=0))
            tick(g.memset(minus_half[:, :], -0.5))
            tick(g.memset(earlier[:, :], 1.0))
            tick(g.memset(minus_sel[:, :, :], 0.0))
            tick(g.memset(tile_mask[:, :], 1.0))
            made()
            tick(g.affine_select(out=minus_sel[:, :, :], in_=minus_sel[:, :, :], compare_op=ALU.not_equal,
                                 fill=-1.0, base=0, pattern=[[-1, H], [0, P]], channel_multiplier=1))
            tick(g.tensor_copy(vocab_f[:, :], vocab_i[:, :]))
            tick(g.tensor_copy(expert_f[:, :], expert_i[:, :]))
            tick(g.affine_select(out=earlier[:, :], in_=earlier[:, :], compare_op=ALU.is_gt, fill=0.0,
                                 base=0, pattern=[[1, P]], channel_multiplier=-1))
            tick(g.affine_select(out=tile_mask[:, :], in_=tile_mask[:, :], compare_op=ALU.is_ge, fill=0.0,
                                 base=0, pattern=[[-E, 8]], channel_multiplier=1))
            made()
            tick(g.affine_select(out=minus_sel[:, :, :], in_=minus_sel[:, :, :], compare_op=ALU.not_equal,
                                 fill=-1.0, base=-H, pattern=[[-1, H], [0, P]], channel_multiplier=1))
            tick(g.affine_select(out=tile_mask[:, :], in_=tile_mask[:, :], compare_op=ALU.is_ge, fill=0.0,
                                 base=E - 1, pattern=[[E, 8]], channel_multiplier=-1))
            tick(g.tensor_scalar(region[:, :], expert_f[:, :], float(CAP), None, ALU.mult))
            made()
            assert done == POOL_CONSTANTS
            g.wait_ge(S["const_dve"], DVE_CONSTANTS)
            g.dma_start(expert_rows[ZERO_ROW:ZERO_ROW + P, :], zeros[:, :]).then_inc(S["zero_row_out"], 16)

            def step(at):
                b = at(-3)
                if b.live:
                    g.wait_ge(S["slot_dve"], SLOT * b.n + SLOT)
                    for k in range(TOP_K):
                        for t in range(NT):
                            c = k * NT + t
                            g.indirect_dma_start(expert_rows[0:ZERO_ROW, :],
                                                 bass.IndirectOffsetOnAxis(slot_i[b.par][:, c:c + 1], 0),
                                                 xn2[b.par][:, t, :], None).then_inc(scattered[b.par], 16)
                b = at(4)
                if b.live:
                    g.wait_ge(S["stat_dve"], STAT * b.n + STAT)
                    g.tensor_scalar(var_eps[b.par][:, :], moments[b.par][:, :, 1], EPS, None, ALU.add).then_inc(
                        S["rstd_pool"], 1)
                    g.wait_ge(S["rstd_pool"], 2 * b.n + 1)
                    g.tensor_tensor(rstd[b.par][:, :], var_eps[b.par][:, :], minus_half[:, :], ALU.pow).then_inc(
                        S["rstd_pool"], 1)
                b = at(3)
                if b.live:
                    g.wait_ge(S["rest_done"], b.n + 1)
                    g.wait_ge(S["part2_done"], b.n + 1)
                    part = qk_part[b.par]
                    g.tensor_tensor(part[:, :, 2, :], qk_rest[b.par][:, :, :], part[:, :, 1, :],
                                    ALU.subtract).then_inc(S["split_pool"], 1)
                b = at(-2)
                if b.live:
                    g.wait_ge(S["route_dve"], ROUTE * b.n + ROUTE)
                    keep = chosen_all[:, :, bass.ds(NT * b.n, NT), :]
                    g.tensor_copy(keep, chosen[b.par][:, :, :, :]).then_inc(S["chosen_kept"], 1)
                b = at(1)
                if b.live:
                    g.wait_ge(S["scored_dve"], NT * H * b.n + NT * H)
                    wait(g, S["max_mm"], b.n - 1)
                    m, parts = row_max[b.par], max_parts[b.par]
                    g.tensor_copy(parts[:, :, 0:H], m[:, :, :]).then_inc(S["max_split"], 1)
                    g.wait_ge(S["max_split"], 2 * b.n + 1)
                    g.tensor_tensor(parts[:, :, H:2 * H], m[:, :, :], parts[:, :, 0:H], ALU.subtract).then_inc(
                        S["max_split"], 1)
                b = at(-1)
                if b.live:
                    g.wait_ge(S["ln2_dve"], LN2 * b.n + LN2)
                    g.tensor_scalar(var_eps2[:, :], moments2[:, :, 1], EPS, None, ALU.add).then_inc(S["rstd2_pool"], 1)
                    g.wait_ge(S["rstd2_pool"], RSTD2 * b.n + 1)
                    g.tensor_tensor(rstd2[:, :], var_eps2[:, :], minus_half[:, :], ALU.pow).then_inc(
                        S["rstd2_pool"], 1)

            run_steps(g, step)

        @block.scalar
        def _(act):
            act.dma_start(conv_nat[:, :, :], conv_w).then_inc(S["conv_in"], 16)
            with nc.allow_non_contiguous_dma(reason="a 4 KB table, once"):
                act.dma_start(bias_t[:, :], rel_bias[0].rearrange("h r -> r h")).then_inc(S["bias_t_in"], 16)

            def step(at):
                def bias_piece(i):
                    if at(0).n == BIAS_STEP:
                        act.wait_ge(S["bias_ps"], i + 1)
                        act.copy(bias_flat[:, i * 512:(i + 1) * 512], bias_banks[i][:, :]).then_inc(
                            S["bias_done"], 1)

                def exp(b, h):
                    if b.live:
                        act.wait_ge(S["turned_mm"], H * b.n + h + 1)
                        wait(act, S["val_mm"], 2 * b.n - 1 + h // 4)
                        act.activation(probs[:, h, :], ps_turn[h % 2][:, :], ACT.Exp).then_inc(S["exp_done"], 1)

                exp(at(-1), 6)
                exp(at(-1), 7)
                b = at(0)
                if b.live:
                    act.wait_ge(S["max_mm"], b.n + 1)
                    wait(act, S["turned_mm"], H * b.n - H)
                    act.copy(maxT[b.par][0:2 * H, :], max_ps).then_inc(S["maxT_done"], 1)
                b = at(4)
                if b.live:
                    act.wait_ge(S["embed_mm"], b.n + 1)
                    if at(3).live:
                        act.wait_ge(S["xnT_mm"], at(3).n + 1)
                    h = hres[:, bass.ds(NT * b.n, NT), :].rearrange("p t d -> p (t d)")
                    act.activation(h, emb_ps, ACT.Relu).then_inc(S["relu_done"], 1)
                b = at(3)
                if b.live:
                    act.wait_ge(S["xnT_mm"], b.n + 1)
                    wait(act, S["v_mm"], b.n - 1)
                    act.copy(xnT[b.par][:, :], xnT_ps).then_inc(S["xnT_done"], 1)
                exp(at(0), 0)
                b = at(3)
                if b.live:
                    act.wait_ge(S["qk_mm"], b.n + 1)
                    wait(act, stacked[b.par], 32 * len(TERMS) * b.half)
                    act.copy(qk_part[b.par][:, :, 0, :], qk_ps.rearrange("p (s t) -> p s t", s=2)).then_inc(
                        S["part1_done"], 1)
                b = at(-2)
                if b.live:
                    act.wait_ge(S["xn2T_mm"], b.n + 1)
                    wait(act, S["logit_mm"], b.n)
                    act.copy(xn2T[:, :], xn2T_ps).then_inc(S["xn2T_done"], 1)
                b = at(-1)
                if b.live:
                    act.wait_ge(S["val_mm"], 2 * b.n + 2)
                    wait(act, S["o_mm"], b.n)
                    act.copy(oT[:, :], ps_val[:, :]).then_inc(S["oT_done"], 1)
                exp(at(0), 1)
                bias_piece(1)
                if at(0).n == BATCH:
                    zero_sums(act, 5, ZERO_PARTS)
                b = at(4)
                exp(at(0), 2)
                if b.live:
                    act.wait_ge(S["w1_mm"], b.n + 1)
                    act.copy(w1T[:, bass.ds(2 * P * b.n, 2 * P)], w1_ps).then_inc(S["w1_done"], 1)
                exp(at(0), 3)
                bias_piece(3)
                b = at(3)
                if b.live:
                    act.wait_ge(S["rest_done"], b.n + 1)
                    act.copy(qk_part[b.par][:, :, 1, :], qk_rest[b.par][:, :, :]).then_inc(S["part2_done"], 1)
                b = at(3)
                if b.live:
                    act.wait_ge(S["v_mm"], b.n + 1)
                    wait(act, S["val_mm"], 2 * b.n - 6)
                    act.copy(v_op[b.quarter][:, :, :, 0:HD],
                             v_ps.rearrange("p (t h d) -> p t h d", t=NT, d=HD)).then_inc(S["v_done"], 1)
                exp(at(0), 4)
                exp(at(0), 5)
                bias_piece(5)

            run_steps(act, step)
            finish_scalar(act)

        @block.vector
        def _(v):
            v.memset(zeros[:, :], 0.0).then_inc(S["const_dve"], 1)
            v.memset(onesf[:, :], 1.0).then_inc(S["const_dve"], 1)
            v.memset(onesb[:, :], 1.0).then_inc(S["const_dve"], 1)
            for i in range(4):
                v.memset(v_op[i][:, :, :, HD + 1:VW], 0.0).then_inc(S["const_dve"], 1)
                v.memset(v_op[i][:, :, :, HD:HD + 1], 1.0).then_inc(S["const_dve"], 1)
            for i in range(2):
                v.memset(maxT[i][:, :], 0.0).then_inc(S["const_dve"], 1)
                v.memset(onehot[i][:, 0:1], 0.0).then_inc(S["const_dve"], 1)
            v.memset(before[0][:, 0, :], 0.0).then_inc(S["const_dve"], 1)
            v.wait_ge(S["conv_in"], 16)
            v.wait_ge(S["const_pool"], GROUPS_MADE)
            for k in range(CONTEXT):
                tap = conv_nat[:, :, k].unsqueeze(1).broadcast_to([P, P // GROUP, GROUP])
                v.tensor_tensor(conv_wide[:, k, :].rearrange("p (g c) -> p g c", c=GROUP),
                                group_mask[:, :].rearrange("p (g c) -> p g c", c=GROUP), tap, ALU.mult).then_inc(
                    S["setup_dve"], 1)
            v.wait_ge(S["setup_pe"], 1)
            for i in range(2):
                v.tensor_scalar(wqkT[:, i, :].rearrange("p (d h) -> p d h", h=H),
                                bank_a[:, i * P:(i + 1) * P].rearrange("p (h d) -> p d h", h=H),
                                HD ** -0.5 if i == 0 else 1.0, None, ALU.mult).then_inc(S["setup_dve"], 1)
            v.tensor_copy(wvT[:, :], bank_a[:, 2 * P:3 * P]).then_inc(S["setup_dve"], 1)
            v.tensor_copy(gateT[:, :], bank_a[:, 3 * P:3 * P + E]).then_inc(S["setup_dve"], 1)
            v.tensor_copy(embT[:, :], bank_b[:, 0:VOCAB]).then_inc(S["setup_dve"], 1)
            v.tensor_copy(convT[:, :, :], bank_b[:, P:3 * P].rearrange("p (k o) -> p k o", k=CONTEXT)).then_inc(
                S["setup_dve"], 1)
            v.wait_ge(S["setup_pe"], 2)
            v.tensor_copy(table[0:VOCAB, :, :], bank_c[0:VOCAB, 0:2 * D].rearrange("p (k o) -> p k o", k=CONTEXT)
                          ).then_inc(S["table_done"], 1)
            rev = bank_c[0:H, 2 * D:2 * D + NREL]
            lead = 2 * P - WINDOW
            v.tensor_copy(bias_ext[:, lead:lead + NREL], rev).then_inc(S["bias_row"], 1)
            v.tensor_copy(bias_ext[:, 0:lead], rev[:, 0:1].broadcast_to([H, lead])).then_inc(S["bias_row"], 1)
            tail = 512 - lead - NREL
            v.tensor_copy(bias_ext[:, 512 - tail:512], rev[:, NREL - 1:NREL].broadcast_to([H, tail])).then_inc(
                S["bias_row"], 1)
            v.wait_ge(S["const_pool"], POOL_CONSTANTS)
            for c in range(2):
                v.tensor_scalar(block_k[:, c:c + 1], vocab_f[:, :], float(P * c), None, ALU.add).then_inc(
                    S["block_k_done"], 1)

            def step(at):
                def bias_piece(i):
                    if at(0).n == BIAS_STEP:
                        v.wait_ge(S["bias_ps"], i + 1)
                        v.tensor_copy(bias_flat[:, i * 512:(i + 1) * 512], bias_banks[i][:, :]).then_inc(
                            S["bias_done"], 1)

                def score(h, t):
                    b = at(1)
                    if b.live:
                        if t == 0:
                            v.wait_ge(S["scores_mm"], H * b.n + h + 1)
                            wait(v, S["turned_mm"], H * b.n - 2 * H + h + 1)
                            if h == 0:
                                wait(v, S["max_split"], 2 * b.n - 2)
                        u = P - P * t
                        v.tensor_tensor_reduce(scored[:, b.par, h, t * T:(t + 1) * T],
                                               ps_score[h % 2][:, t * T:(t + 1) * T], bias[:, h, u:u + T],
                                               1.0, LOW, ALU.add, ALU.max,
                                               row_max[b.par][:, t, h:h + 1]).then_inc(S["scored_dve"], 1)

                def tile_of(b, t):
                    return hres[:, bass.ds(NT * b.n + t, 1), :].rearrange("p t d -> p (t d)")

                if at(1).n == 0:
                    v.wait_ge(S["bias_done"], 6)
                score(0, 0)
                place(v, at(-3), 0)
                score(0, 1)
                b = at(4)
                if b.live:
                    v.wait_ge(tok_in[b.par], 16 * b.half + 16)
                    wait(v, S["embed_mm"], b.n - 1)
                    v.tensor_scalar(onehot[b.par][:, 1:1 + T], tok[b.par][:, :], float(VOCAB - 1), vocab_f[:, 0:1],
                                    ALU.min, ALU.is_equal).then_inc(S["onehot_done"], 1)
                place(v, at(-3), 1)
                b = at(-2)
                if b.live:
                    wait(v, S["xn2_done"], NT * b.n)
                    v.wait_ge(S["rstd2_pool"], RSTD2 * b.n + RSTD2)
                    wait(v, scattered[b.par], 16 * TOP_K * NT * b.half)
                    wait(v, S["xn2T_mm"], b.n - 1)
                    for t in range(NT):
                        v.tensor_scalar(xn2[b.par][:, t, :], tile_of(b, t), moments2[:, t, 0:1],
                                        rstd2[:, t:t + 1], ALU.subtract, ALU.mult).then_inc(S["xn2_done"], 1)
                score(1, 0)
                place(v, at(-3), 2)
                score(1, 1)
                place(v, at(-3), 3)
                score(2, 0)
                score(2, 1)
                b = at(3)
                if b.live:
                    v.wait_ge(S["part1_done"], b.n + 1)
                    wait(v, S["split_pool"], b.n - 1)
                    v.tensor_tensor(qk_rest[b.par][:, :, :], qk_ps.rearrange("p (s t) -> p s t", s=2),
                                    qk_part[b.par][:, :, 0, :], ALU.subtract).then_inc(S["rest_done"], 1)
                if at(0).n == BATCH + 1:
                    zero_sums(v, 0, 5)
                score(3, 0)
                b = at(4)
                if b.live:
                    v.wait_ge(S["relu_done"], b.n + 1)
                    wait(v, S["xn_done"], NT * b.n - NT)
                    for t in range(NT):
                        v.bn_stats(stats[b.par][:, t, :], tile_of(b, t)).then_inc(S["stat_dve"], 1)
                score(3, 1)
                if b.live:
                    v.wait_ge(S["stat_dve"], STAT * b.n + NT)
                    for t in range(NT):
                        v.bn_aggr(moments[b.par][:, t, :], stats[b.par][:, t, :]).then_inc(S["stat_dve"], 1)
                score(4, 0)
                bias_piece(0)
                score(4, 1)
                route_logits(v, at(-2))
                score(5, 0)
                route_largest(v, at(-2))
                if b.live:
                    v.wait_ge(S["rstd_pool"], 2 * b.n + 2)
                    wait(v, S["xnT_mm"], b.n - 1)
                    for t in range(NT):
                        v.tensor_scalar(xn[b.par][:, t, :], tile_of(b, t), moments[b.par][:, t, 0:1],
                                        rstd[b.par][:, t:t + 1], ALU.subtract, ALU.mult).then_inc(S["xn_done"], 1)
                bias_piece(2)
                score(5, 1)
                route_index(v, at(-2))
                b = at(-1)
                if b.live:
                    v.wait_ge(S["o_mm"], b.n + 1)
                    o = o_ps.rearrange("p (c w) -> p c w", w=VW)
                    wait(v, S["o_norm_done"], b.n)
                    v.reciprocal(o_rec[:, :].unsqueeze(2), o[:, :, HD:HD + 1]).then_inc(S["o_chain"], 1)
                score(6, 0)
                route_choice(v, at(-2))
                if b.live:
                    v.wait_ge(S["o_chain"], b.n + 1)
                    wait(v, S["hres_done"], b.n)
                    v.tensor_tensor(o_norm[:, :, :].rearrange("p t (h d) -> p (t h) d", d=HD), o[:, :, 0:HD],
                                    o_rec[:, :].unsqueeze(2).broadcast_to([P, NT * H, HD]), ALU.mult).then_inc(
                        S["o_norm_done"], 1)
                score(6, 1)
                route_mask(v, at(-2))
                if b.live:
                    v.wait_ge(S["o_norm_done"], b.n + 1)
                    h = hres[:, bass.ds(NT * b.n, NT), :]
                    v.tensor_tensor(h, h, o_norm[:, :, :], ALU.add).then_inc(S["hres_done"], 1)
                bias_piece(4)
                score(7, 0)
                route_count(v, at(-2), 0)
                if b.live:
                    v.wait_ge(S["hres_done"], b.n + 1)
                    wait(v, S["xn2_done"], NT * b.n)
                    for t in range(NT):
                        v.bn_stats(stats2[:, t, :], tile_of(b, t)).then_inc(S["ln2_dve"], 1)
                score(7, 1)
                route_count(v, at(-2), 1)
                if b.live:
                    v.wait_ge(S["ln2_dve"], LN2 * b.n + NT)
                    for t in range(NT):
                        v.bn_aggr(moments2[:, t, :], stats2[:, t, :]).then_inc(S["ln2_dve"], 1)

            run_steps(v, step)
            finish_vector(v)

        @block.tensor
        def _(pe):
            pe.wait_ge(S["const_pool"], IDENT_MADE)
            pe.wait_ge(S["weights_in"], 80)
            for i in range(3):
                pe.transpose(bank_a[:, i * P:(i + 1) * P], w_nat[:, i, :], ident[:, :])
            pe.transpose(bank_a[:, 3 * P:3 * P + E], gate_nat[:, :], ident[0:E, 0:E])
            pe.transpose(bank_b[:, 0:VOCAB], emb_nat[:, :], ident[0:VOCAB, 0:VOCAB])
            pe.wait_ge(S["setup_dve"], CONTEXT)
            for k in range(CONTEXT):
                mm = pe.transpose(bank_b[:, (k + 1) * P:(k + 2) * P], conv_wide[:, k, :], ident[:, :])
            mm.then_inc(S["setup_pe"], 1)
            pe.wait_ge(S["setup_dve"], CONTEXT + 6)
            for k in range(CONTEXT):
                pe.matmul(bank_c[0:VOCAB, k * D:(k + 1) * D], embT[:, :], convT[:, k, :], start=True, stop=True)
            pe.wait_ge(S["bias_t_in"], 16)
            pe.matmul(bank_c[0:H, 2 * D:2 * D + NREL], bias_t[:, :], anti[0:NREL, 1:P], start=True,
                      stop=True).then_inc(S["setup_pe"], 1)
            pe.wait_ge(S["table_done"], 1)
            pe.wait_ge(S["const_pool"], POOL_CONSTANTS)
            pe.wait_ge(S["const_dve"], DVE_CONSTANTS)

            def step(at):
                def bias_piece(i):
                    if at(0).n != BIAS_STEP:
                        return
                    pe.wait_ge(S["bias_wide"], 16)
                    pe.wait_ge(S["bias_row"], 3)
                    h, u = divmod(i * 512, BIASW)
                    done = 0
                    while done < 512:
                        n = min(BIASW - u, 512 - done)
                        mm = pe.matmul(bias_banks[i][:, done:done + n], anti[:, :], probs[:, h, u:u + n],
                                       start=True, stop=True)
                        done, u, h = done + n, 0, h + 1
                    mm.then_inc(S["bias_ps"], 1)

                def score(h):
                    b = at(1)
                    if b.live:
                        if h == 0:
                            pe.wait_ge(stacked[b.par], 32 * len(TERMS) * b.half + 32 * len(TERMS))
                        wait(pe, S["scored_dve"], NT * (H * b.n + h - 1))
                        st = stack[b.par]
                        for t in range(NT):
                            mm = pe.matmul(ps_score[h % 2][:, t * T:(t + 1) * T], st[:, 0, h, t * P:(t + 1) * P],
                                           st[:, 1, h, :], start=True, stop=True)
                        mm.then_inc(S["scores_mm"], 1)

                def turn(b, h):
                    if not b.live:
                        return
                    wait(pe, S["exp_done"], H * b.n + h - 1)
                    pe.wait_ge(S["scored_dve"], NT * (H * b.n + h + 1))
                    bank = ps_turn[h % 2]
                    for j in range(NT):
                        for t in range(NT):
                            pe.matmul(bank[:, j * T + t * P:j * T + (t + 1) * P],
                                      scored[:, b.par, h, t * T + j * P:t * T + (j + 1) * P], ident[:, :],
                                      start=(j + t == 0), stop=False, is_transpose=True, skip_group_check=True)
                    if h == 0:
                        pe.wait_ge(S["maxT_done"], b.n + 1)
                    pe.matmul(bank[:, :].rearrange("p (j t) -> p j t", j=NT), minus_sel[:, h, :],
                              maxT[b.par][:, :].unsqueeze(1).broadcast_to([P, NT, T]),
                              start=False, stop=True, skip_group_check=True).then_inc(S["turned_mm"], 1)

                def values(b, group):
                    if not b.live:
                        return
                    pe.wait_ge(S["exp_done"], H * b.n + 4 * group + 4)
                    pe.wait_ge(S["v_done"], b.n + 1)
                    if group == 0:
                        wait(pe, S["oT_done"], b.n)
                    for j in range(NT):
                        for q in range(4):
                            h = 4 * group + q
                            mm = pe.matmul(ps_val[VW * q:VW * (q + 1), group * T:(group + 1) * T],
                                           v_op[b.quarter][:, j, h, :], probs[:, h, j * T:(j + 1) * T],
                                           start=(j == 0), stop=(j == NT - 1))
                    mm.then_inc(S["val_mm"], 1)

                if at(1).n == 0:
                    pe.wait_ge(S["bias_done"], 6)
                score(0)
                turn(at(-1), 6)
                score(1)
                turn(at(-1), 7)
                b = at(0)
                if b.live:
                    pe.wait_ge(S["max_split"], 2 * b.n + 2)
                    if at(-3).live:
                        wait(pe, S["slot_dve"], SLOT * at(-3).n + 1)
                    for t in range(NT):
                        mm = pe.transpose(max_ps[:, t * P:(t + 1) * P], max_parts[b.par][:, t, :], identb[:, :])
                    mm.then_inc(S["max_mm"], 1)
                b = at(4)
                if b.live:
                    pe.wait_ge(S["onehot_done"], b.n + 1)
                    wait(pe, S["v_done"], b.n - 1)
                    wait(pe, S["w1_done"], b.n)
                    for t in range(NT):
                        for k in range(CONTEXT):
                            mm = pe.matmul(emb_ps[:, t * D:(t + 1) * D],
                                           onehot[b.par][0:VOCAB, t * P + k:t * P + k + P], table[0:VOCAB, k, :],
                                           start=(k == 0), stop=(k == CONTEXT - 1))
                    mm.then_inc(S["embed_mm"], 1)
                b = at(3)
                if b.live:
                    pe.wait_ge(S["xn_done"], NT * b.n + NT)
                    wait(pe, S["v_done"], b.n)
                    pe.wait_ge(S["w1_done"], b.n + 1)
                    for t in range(NT):
                        mm = pe.transpose(xnT_ps[:, t * P:(t + 1) * P], xn[b.par][:, t, :], ident[:, :])
                    mm.then_inc(S["xnT_mm"], 1)
                bias_piece(0)
                score(2)
                turn(at(0), 0)
                b = at(3)
                if b.live:
                    pe.wait_ge(S["xnT_done"], b.n + 1)
                    prev = at(-2)
                    if prev.live:
                        pe.wait_ge(S["o_norm_done"], prev.n + 1)
                    for side in range(2):
                        mm = pe.matmul(qk_ps[:, side * T:(side + 1) * T], wqkT[:, side, :], xnT[b.par][:, :],
                                       start=True, stop=True)
                    mm.then_inc(S["qk_mm"], 1)
                b = at(-2)
                if b.live:
                    pe.wait_ge(S["xn2_done"], NT * b.n + NT)
                    if at(0).live:
                        pe.wait_ge(S["maxT_done"], at(0).n + 1)
                    elif at(-3).live:
                        pe.wait_ge(S["slot_dve"], SLOT * at(-3).n + 1)
                    for t in range(NT):
                        mm = pe.transpose(xn2T_ps[:, t * P:(t + 1) * P], xn2[b.par][:, t, :], ident[:, :])
                    mm.then_inc(S["xn2T_mm"], 1)
                bias_piece(1)
                values(at(-1), 1)
                score(3)
                turn(at(0), 1)
                b = at(-2)
                if b.live:
                    pe.wait_ge(S["xn2T_done"], b.n + 1)
                    for t in range(NT):
                        mm = pe.matmul(logit_ps[:, t * E:(t + 1) * E], xn2T[:, t * P:(t + 1) * P], gateT[:, :],
                                       start=True, stop=True)
                    mm.then_inc(S["logit_mm"], 1)
                bias_piece(2)
                b = at(4)
                if b.live:
                    pe.wait_ge(w1_loaded[b.par], 16 * b.half + 16)
                    pe.wait_ge(S["relu_done"], b.n + 1)
                    prev = at(3)
                    if prev.live:
                        pe.wait_ge(S["xnT_done"], prev.n + 1)
                    for t in range(2):
                        mm = pe.transpose(w1_ps[:, t * P:(t + 1) * P], w1_in[b.par][:, t, :], ident[:, :])
                    mm.then_inc(S["w1_mm"], 1)
                score(4)
                turn(at(0), 2)
                bias_piece(3)
                b = at(-1)
                if b.live:
                    pe.wait_ge(S["oT_done"], b.n + 1)
                    other = at(3)
                    if other.live:
                        pe.wait_ge(S["part1_done"], other.n + 1)
                        pe.wait_ge(S["rest_done"], other.n + 1)
                    for t in range(NT):
                        for group in range(2):
                            c = t * 2 + group
                            mm = pe.transpose(o_ps[:, c * P:(c + 1) * P],
                                              oT[:, group * T + t * P:group * T + (t + 1) * P], ident[:, :])
                    mm.then_inc(S["o_mm"], 1)
                score(5)
                turn(at(0), 3)
                bias_piece(4)
                b = at(3)
                if b.live:
                    other = at(4)
                    if other.live:
                        pe.wait_ge(S["w1_done"], other.n + 1)
                    for t in range(NT):
                        mm = pe.matmul(v_ps[:, t * D:(t + 1) * D], xnT[b.par][:, t * P:(t + 1) * P], wvT[:, :],
                                       start=True, stop=True)
                    mm.then_inc(S["v_mm"], 1)
                score(6)
                turn(at(0), 4)
                bias_piece(5)
                score(7)
                turn(at(0), 5)
                values(at(0), 0)
                b = at(-2)
                if b.live:
                    pe.wait_ge(S["route_dve"], ROUTE * b.n + ROUTE)
                    pe.wait_ge(S["count_dve"], COUNT * b.n + 1)
                    for t in range(NT):
                        pe.matmul(rank_ps[:, t * E:(t + 1) * E], earlier[:, :], mask[b.par][:, t, :],
                                  start=True, stop=False)
                        mm = pe.matmul(rank_ps[:, t * E:(t + 1) * E], onesb[:, :], before[b.par][:, t, :],
                                       start=False, stop=True)
                    mm.then_inc(S["rank_mm"], 1)

            run_steps(pe, step)
            finish_tensor(pe)


_INS = ["x", "L0_tok_emb_table", "L0_tok_conv_w", "L0_attn_Wq", "L0_attn_Wk", "L0_attn_Wv", "L0_attn_rel_pos_bias",
        "L0_ffn_gate_weight", "L0_ffn_w1", "L0_ffn_w2"]


def kernel(**inputs):
    import numpy as _np
    import concourse.bacc as _bacc
    from concourse import mybir as _mybir
    from concourse.bass_utils import run_bass_kernel_spmd as _run

    nc = _bacc.Bacc("TRN2", target_bir_lowering=False, num_devices=1)
    arrays, args = {}, []
    for name in _INS:
        a = _np.ascontiguousarray(inputs[name])
        arrays[f"in_{name}"] = a
        args.append(nc.dram_tensor(f"in_{name}", a.shape, _mybir.dt.from_np(a.dtype), kind="ExternalInput").ap())
    out = nc.dram_tensor("out_0", (BATCH, T, D), _mybir.dt.float32, kind="ExternalOutput").ap()
    tower_kernel(nc, *args, out)
    r = _run(nc, [arrays], core_ids=[0])
    return r.results[0]["out_0"]
```

```python
from contextlib import ExitStack

import concourse.bass as bass
from concourse import mybir

F32 = mybir.dt.float32
BF16 = mybir.dt.bfloat16
I32 = mybir.dt.int32
U32 = mybir.dt.uint32
ALU = mybir.AluOpType
ACT = mybir.ActivationFunctionType
AX = mybir.AxisListType

P = 128
BATCH, T, D = 32, 256, 128
NT = T // P
TILES = BATCH * NT
H, HD = 8, 16
VW = 32
VOCAB, CONTEXT, GROUP = 125, 2, 4
WINDOW = 64
NREL = 2 * WINDOW - 1
BIASW = NT * P + P
E, F = 16, 512
TOP_K = 2
CAP = BATCH * T + P
ZERO_ROW = E * CAP
UNROLL = 8
AHEAD = 2
TURNS = -(-(BATCH * T * TOP_K // P + E - 1) // UNROLL)
BLOCKS = TURNS * UNROLL
ZERO_PARTS = 16
QUAD = 32
EPS = 1e-5
LOW = -3.0e38
TERMS = [(0, 0), (0, 1), (1, 0), (1, 1), (0, 2), (2, 0)]
KROWS = len(TERMS) * HD
CENTERED_FROM = 4
CENTERED = H - CENTERED_FROM
POOL_CONSTANTS, DVE_CONSTANTS = 23, 16
IDENT_MADE, GROUPS_MADE = 7, 9
FIRST_STEP, LAST_STEP = -6, BATCH + 2
LOOP_FROM, LOOP_TO = 4, 28
BIAS_STEP = -2


def settled(eng, passed, b):
    if not isinstance(b.n, int):
        eng.sem_inc(passed, 1)


class Batch:

    def __init__(self, quad, off, in_loop):
        self.n = off + 4 * quad
        self.par = off % 2
        self.quarter = off % 4
        self.half = off // 2 + 2 * quad
        self.live = in_loop or 0 <= off < BATCH


def run_steps(eng, step, loop_to=LOOP_TO):
    for s in range(FIRST_STEP, LOOP_FROM):
        step(lambda d: Batch(0, s + d, False))
    with eng.Fori(LOOP_FROM // 4, loop_to // 4) as quad:
        for u in range(4):
            step(lambda d: Batch(quad, u + d, True))
    for s in range(loop_to, LAST_STEP + 1):
        step(lambda d: Batch(0, s + d, False))


def written_out(batch, n):
    return isinstance(batch.n, int) and batch.n == n


def run_turns(eng, turn):
    turn(0)
    with eng.Fori(1, TURNS - 1) as i:
        turn(i)
    turn(TURNS - 1)


def wait(eng, semaphore, count):
    if not isinstance(count, int) or count > 0:
        eng.wait_ge(semaphore, count)


def tower_kernel(nc, x, emb, conv_w, wq, wk, wv, rel_bias, gate_w, w1, w2, out):
    with ExitStack() as ctx:
        def sb(name, shape, dt=F32):
            return ctx.enter_context(nc.sbuf_tensor(name, shape, dt))

        def pb(name, shape=(P, 512), dt=F32):
            return ctx.enter_context(nc.psum_tensor(name, list(shape), dt))

        def sem(name):
            return ctx.enter_context(nc.semaphore(name))

        expert_rows = nc.dram_tensor("expert_rows", (ZERO_ROW + P, D), F32)
        bias_rows = nc.dram_tensor("bias_rows", (H, 512), F32)

        ident = sb("ident", [P, P])
        identb = sb("identb", [P, P], BF16)
        anti = sb("anti", [P, P])
        onesf = sb("onesf", [P, P])
        onesb = sb("onesb", [P, P], BF16)
        earlier = sb("earlier", [P, P], BF16)
        minus_sel = sb("minus_sel", [P, H, P], BF16)
        group_mask = sb("group_mask", [P, P])
        tile_mask = sb("tile_mask", [P, 8])
        vocab_i = sb("vocab_i", [P, 1], I32)
        vocab_f = sb("vocab_f", [P, 1])
        expert_i = sb("expert_i", [P, E], I32)
        expert_f = sb("expert_f", [P, E])
        region = sb("region", [P, E])
        minus_half = sb("minus_half", [P, NT])
        zeros = sb("zeros", [P, P])
        w_nat = sb("w_nat", [P, 3, P])
        gate_nat = sb("gate_nat", [E, D])
        emb_nat = sb("emb_nat", [VOCAB, D])
        conv_nat = sb("conv_nat", [P, GROUP, CONTEXT])
        bias_t = sb("bias_t", [NREL, H])
        conv_wide = sb("conv_wide", [P, CONTEXT, P])
        wqkT = sb("wqkT", [P, 2, P])
        wvT = sb("wvT", [P, P])
        gateT = sb("gateT", [P, E])
        embT = sb("embT", [P, VOCAB])
        convT = sb("convT", [P, CONTEXT, P])
        table = sb("table", [P, 3, CONTEXT, D], BF16)
        table_rest = sb("table_rest", [P, CONTEXT, D])
        bias_ext = sb("bias_ext", [H, 512])
        arena = sb("arena", [P, E * F])
        stack_cols = 2 * H * T // 2
        stack = [arena[0:KROWS, i * stack_cols:(i + 1) * stack_cols].bitcast(BF16).rearrange(
            "p (s h t) -> p s h t", s=2, h=H) for i in range(2)]
        bias_at, rest_at = 2 * stack_cols, 2 * stack_cols + H * BIASW
        bias_flat = arena[:, bias_at:rest_at]
        bias = bias_flat.rearrange("p (h u) -> p h u", h=H)
        qk_rest = [arena[:, rest_at + i * 2 * T:rest_at + (i + 1) * 2 * T].rearrange(
            "p (s t) -> p s t", s=2) for i in range(2)]
        w2_in_quads = arena[:, :].rearrange("p (a f) -> p a f", a=E)
        w1_in = [sb(f"w1_in{i}", [P, 2, D]) for i in range(2)]
        w1T = sb("w1T", [P, E * F])
        tok = [sb(f"tok{i}", [P, T], I32) for i in range(2)]
        onehot = [sb(f"onehot{i}", [P, 1 + T], BF16) for i in range(2)]
        hres = sb("hres", [P, TILES, D])
        stats = [sb(f"stats{i}", [P, NT, 6]) for i in range(2)]
        moments = [sb(f"moments{i}", [P, NT, 2]) for i in range(2)]
        var_eps = [sb(f"var_eps{i}", [P, NT]) for i in range(2)]
        rstd = [sb(f"rstd{i}", [P, NT]) for i in range(2)]
        xn = [sb(f"xn{i}", [P, NT, D]) for i in range(2)]
        xnT = [sb(f"xnT{i}", [P, T]) for i in range(2)]
        qk_part = [sb(f"qk_part{i}", [P, 2, 3, T], BF16) for i in range(2)]
        v_op = [sb(f"v_op{i}", [P, NT, H, VW]) for i in range(4)]
        scored = sb("scored", [P, 2, H, NT * T])
        row_max = [sb(f"row_max{i}", [P, NT, H]) for i in range(2)]
        minus_max = [sb(f"minus_max{i}", [P, NT, CENTERED]) for i in range(2)]
        max_parts = [sb(f"max_parts{i}", [P, NT, 2 * H], BF16) for i in range(2)]
        maxT = [sb(f"maxT{i}", [P, T], BF16) for i in range(2)]
        probs = sb("probs", [P, H, NT * T])
        oT = sb("oT", [P, 2 * T])
        o_rec = sb("o_rec", [P, NT * H])
        o_norm = sb("o_norm", [P, NT, D])
        stats2 = sb("stats2", [P, NT, 6])
        moments2 = sb("moments2", [P, NT, 2])
        var_eps2 = sb("var_eps2", [P, NT])
        rstd2 = sb("rstd2", [P, NT])
        xn2 = [sb(f"xn2_{i}", [P, NT, D]) for i in range(2)]
        xn2T = sb("xn2T", [P, T])
        logits = sb("logits", [P, NT, E])
        largest = sb("largest", [P, NT, 8])
        largest_at = sb("largest_at", [P, NT, 8], U32)
        chosen = [sb(f"chosen{i}", [P, TOP_K, NT, E]) for i in range(2)]
        mask = [sb(f"mask{i}", [P, NT, E], BF16) for i in range(2)]
        before = [sb(f"before{i}", [P, NT, E], BF16) for i in range(2)]
        slot = sb("slot", [P, NT, E])
        slot_of = sb("slot_of", [P, TOP_K, NT, E])
        slot_f = sb("slot_f", [P, TOP_K * NT])
        slot_i = [sb(f"slot_i{i}", [P, TOP_K * NT], I32) for i in range(2)]
        gap_all = sb("gap_all", [P, TILES])
        chosen_all = sb("chosen_all", [P, TOP_K, TILES, E], BF16)

        sums = scored[:, :, :, :].rearrange("p a h t -> p (a h t)")
        hidden = [probs[:, i, :] for i in range(2)]
        block_rows = [probs[:, 2, i * D:(i + 1) * D] for i in range(4)] + [
            xnT[i // 2][:, (i % 2) * D:(i % 2 + 1) * D] for i in range(4)]
        y_prod = [probs[:, 6 + i, :] for i in range(2)]
        blockT = [probs[:, 5, i * P:(i + 1) * P] for i in range(4)]
        counts = sb("counts", [P, E])
        counts1 = sb("counts1", [P, E])
        per_token = sb("per_token", [P, E])
        end_i = sb("end_i", [P, E], I32)
        blocks_i = sb("blocks_i", [P, E], I32)
        blocks_s = sb("blocks_s", [P, E], I32)
        blocks = sb("blocks", [P, E])
        block_end = sb("block_end", [P, E])
        block_k = sb("block_k", [P, 2])
        passed = w_nat[:, 1, 0:2 * E].rearrange("p (c e) -> p c e", c=2)
        passed_blocks = w_nat[:, 1, 2 * E:4 * E].rearrange("p (c e) -> p c e", c=2)
        plan_e = sb("plan_e", [P, 2])
        plan_b = sb("plan_b", [P, 2])
        plan_l = sb("plan_l", [P, 2])
        plan_f = sb("plan_f", [P, 4])
        plan_i = sb("plan_i", [1, 4 * P], I32)
        gap_exp = sb("gap_exp", [P, TILES])
        gap_exp1 = sb("gap_exp1", [P, TILES])
        share = sb("share", [P, TOP_K, TILES])
        gates_k = arena[:, E * F - TOP_K * TILES * E:E * F].rearrange("p (k t e) -> p k t e", k=TOP_K, e=E)
        gates = sb("gates", [P, TILES, E])
        gateT_all = probs[:, 3:5, :].rearrange("p a (g t) -> p (a g) t", t=P)
        yT = sb("yT", [P, E])
        y_parts = probs[:, 5, :].rearrange("p (a m) -> p a m", a=4)
        d_of = w_nat[:, 2, 0:QUAD]
        quad_of = w_nat[:, 2, QUAD:QUAD + 4]
        mean_of = w_nat[:, 2, QUAD + 4:QUAD + 4 + E]
        y_block = gates[:, :, :].rearrange("p (t a) e -> p t (a e)", t=8)

        ps_score = [pb(f"ps_score{i}") for i in range(2)]
        ps_turn = [pb(f"ps_turn{i}") for i in range(2)]
        ps_val = pb("ps_val")
        bank_a, bank_b, bank_c = pb("bank_a"), pb("bank_b"), pb("bank_c")
        emb_ps, xnT_ps = bank_a[:, 0:T], bank_a[:, T:2 * T]
        v_ps, w1_ps = bank_a[:, 0:T], bank_a[:, T:2 * T]
        qk_ps = bank_b[:, :]
        o_ps = bank_b[:, :]
        xn2T_ps = bank_c[:, 0:T]
        max_ps = bank_c[0:2 * H, T:T + P].bitcast(BF16)
        logit_ps = bank_c[:, 384:384 + NT * E]
        rank_ps = bank_c[:, 416:416 + NT * E]

        bias_banks = ps_score + ps_turn + [ps_val, bank_c]
        up_ps = ps_score + ps_turn
        turn_ps = [bank[:, 0:P] for bank in (bank_a, bank_b, bank_c, ps_val)]

        names = """plan_done padded block_turned result_done stored sums_zero gap_exp_done gate_mm gateT_done up_mm summed
        silu_done plan_dve plan_ready plan_mm count_mm gates_done blockT_done spread_mm y_done y_wide_done
        y_mm y_block_done mix_mm weights_in conv_in bias_t_in bias_in bias_row bias_wide const_pool
        const_dve setup_pe setup_dve table_done block_k_done bias_ps bias_done w2_in zero_row_out
        onehot_done embed_mm relu_done stat_dve rstd_pool xn_done xnT_mm xnT_done w1_mm w1_done qk_mm
        part1_done rest_done split_pool part2_done v_mm v_done scores_mm scored_dve max_split minus_max_done
        centered max_mm maxT_done turned_mm exp_done val_mm oT_done o_mm o_chain o_norm_done hres_done
        ln2_dve rstd2_pool xn2_done xn2T_mm xn2T_done logit_mm route_dve gap_done chosen_kept count_dve
        rank_mm slot_dve""".split()
        names += ["vector_passed", "pool_passed"]
        S = {n: sem(n) for n in names}
        tok_in = [sem(f"tok_in{i}") for i in range(2)]
        w1_loaded = [sem(f"w1_loaded{i}") for i in range(2)]
        scattered = [sem(f"scattered{i}") for i in range(2)]
        block_in = [sem(f"block_in{i}") for i in range(UNROLL)]
        stacked = [sem(f"stacked{i}") for i in range(2)]
        STAT, LN2, RSTD2, ROUTE, COUNT, SLOT = 4, 4, 2, 8, 2, 4

        SP, PE, DVE = mybir.EngineType.SP, mybir.EngineType.PE, mybir.EngineType.DVE

        def plan_values(engine, at, largest_value):
            for u in range(UNROLL):
                if u % 4 == 0:
                    _, four = nc.values_load_multi_w_load_instructions(
                        plan_i[0:1, bass.ds(at + u, 4)], engines=[engine], min_val=0, max_val=largest_value,
                        skip_runtime_bounds_check_because="the plan comes from counts and is cut to this range")
                yield four[u % 4]

        def zero_ends(eng, engine, half):
            for quad in range(2):
                first = E // 2 * half + 4 * quad
                _, ends = nc.values_load_multi_w_load_instructions(
                    end_i[0:1, first:first + 4], engines=[engine], min_val=0, max_val=ZERO_ROW - P,
                    skip_runtime_bounds_check_because="a region's start and a count of at most every token")
                for end in ends:
                    eng.dma_start(expert_rows[bass.ds(end, P), :], zeros[:, :]).then_inc(S["padded"], 16)

        def zero_sums(eng, first, last):
            eng.wait_ge(S["turned_mm"], H * BATCH)
            for i in range(first, last):
                part = sums[:, i * (E * F // ZERO_PARTS):(i + 1) * (E * F // ZERO_PARTS)]
                if eng is nc.vector:
                    ins = eng.memset(part, 0.0)
                else:
                    ins = eng.copy(part.rearrange("p (a b) -> p a b", b=P),
                                   zeros[:, :].unsqueeze(1).broadcast_to([P, E * F // ZERO_PARTS // P, P]))
                ins.then_inc(S["sums_zero"], 1)

        def route_logits(v, b):
            if b.live:
                v.wait_ge(S["logit_mm"], b.n + 1)
                v.tensor_copy(logits[:, :, :].rearrange("p t e -> p (t e)"), logit_ps).then_inc(S["route_dve"], 1)

        def route_largest(v, b):
            if b.live:
                v.wait_ge(S["route_dve"], ROUTE * b.n + 1)
                settled(v, S["vector_passed"], b)
                for t in range(NT):
                    v.max(largest[:, t, :], logits[:, t, :]).then_inc(S["route_dve"], 1)

        def route_index(v, b):
            if b.live:
                v.wait_ge(S["route_dve"], ROUTE * b.n + 1 + NT)
                settled(v, S["vector_passed"], b)
                for t in range(NT):
                    v.max_index(largest_at[:, t, :], largest[:, t, :], logits[:, t, :]).then_inc(S["route_dve"], 1)

        def route_choice(v, b):
            if b.live:
                v.wait_ge(S["route_dve"], ROUTE * b.n + 1 + 2 * NT)
                for k in range(TOP_K):
                    at = largest_at[:, :, k:k + 1].broadcast_to([P, NT, E])
                    ex = expert_f[:, :].unsqueeze(1).broadcast_to([P, NT, E])
                    v.tensor_tensor(chosen[b.par][:, k, :, :], ex, at, ALU.is_equal).then_inc(S["route_dve"], 1)
                v.tensor_tensor(gap_all[:, bass.ds(NT * b.n, NT)].unsqueeze(2), largest[:, :, 1:2],
                                largest[:, :, 0:1], ALU.subtract).then_inc(S["gap_done"], 1)

        def route_mask(v, b):
            if b.live:
                v.wait_ge(S["route_dve"], ROUTE * b.n + 1 + 2 * NT + TOP_K)
                v.tensor_tensor(mask[b.par][:, :, :], chosen[b.par][:, 0, :, :], chosen[b.par][:, 1, :, :],
                                ALU.add).then_inc(S["route_dve"], 1)

        def route_count(v, b, tile):
            if b.live:
                cur, nxt, m = before[b.par], before[1 - b.par], mask[b.par]
                if tile == 0:
                    v.wait_ge(S["route_dve"], ROUTE * b.n + ROUTE)
                    wait(v, S["count_dve"], COUNT * b.n)
                    v.tensor_tensor(cur[:, 1, :], cur[:, 0, :], m[:, 0, :], ALU.add).then_inc(S["count_dve"], 1)
                else:
                    v.wait_ge(S["count_dve"], COUNT * b.n + 1)
                    v.tensor_tensor(nxt[:, 0, :], cur[:, 1, :], m[:, 1, :], ALU.add).then_inc(S["count_dve"], 1)

        def place(v, b, stage):
            if not b.live:
                return
            if stage == 0:
                v.wait_ge(S["rank_mm"], b.n + 1)
                v.tensor_tensor(slot[:, :, :], rank_ps.rearrange("p (t e) -> p t e", e=E),
                                region[:, :].unsqueeze(1).broadcast_to([P, NT, E]), ALU.add).then_inc(
                    S["slot_dve"], 1)
            if stage == 1:
                v.wait_ge(S["slot_dve"], SLOT * b.n + 1)
                v.tensor_tensor(slot_of[:, :, :, :], chosen[b.par][:, :, :, :],
                                slot[:, :, :].unsqueeze(1).broadcast_to([P, TOP_K, NT, E]), ALU.mult).then_inc(
                    S["slot_dve"], 1)
            if stage == 2:
                v.wait_ge(S["slot_dve"], SLOT * b.n + 2)
                v.tensor_reduce(slot_f[:, :], slot_of[:, :, :, :].rearrange("p k t e -> p (k t) e"), AX.X,
                                ALU.add).then_inc(S["slot_dve"], 1)
            if stage == 3:
                v.wait_ge(S["slot_dve"], SLOT * b.n + 3)
                wait(v, scattered[b.par], 16 * TOP_K * NT * b.half)
                v.tensor_copy(slot_i[b.par][:, :], slot_f[:, :]).then_inc(S["slot_dve"], 1)

        def finish_sync(sp):
            sp.wait_ge(S["plan_done"], 1)
            zero_ends(sp, mybir.EngineType.SP, 0)
            sp.wait_ge(S["zero_row_out"], 16)
            sp.wait_ge(S["padded"], 16 * E)
            for i in range(2):
                sp.wait_ge(scattered[i], 16 * TOP_K * TILES // 2)
            sp.wait_ge(S["val_mm"], 2 * BATCH)
            sp.wait_ge(S["plan_done"], 2)

            def load(turn):
                rows = plan_values(SP, UNROLL * turn, ZERO_ROW)
                for u, row in enumerate(rows):
                    wait(sp, S["block_turned"], UNROLL * turn + u - UNROLL + 1)
                    sp.dma_start(block_rows[u], expert_rows[bass.ds(row, P), :]).then_inc(block_in[u], 16)

            run_turns(sp, load)
            out_v = out.rearrange("b (t p) d -> p (b t) d", p=P)
            for i in range(TILES // 4):
                sp.wait_ge(S["result_done"], i + 1)
                sp.dma_start(out_v[:, 4 * i:4 * i + 4, :], hres[:, 4 * i:4 * i + 4, :]).then_inc(S["stored"], 16)
            sp.wait_ge(S["stored"], 16 * (TILES // 4))

        def finish_gpsimd(g):
            g.wait_ge(S["gates_done"], 1)
            source = w2.rearrange("(q g) (a d) f -> (g a) q d f", q=4, d=QUAD)
            with g.Fori(0, E) as i:
                for q in range(4):
                    g.dma_start(w2_in_quads[QUAD * q:QUAD * (q + 1), bass.ds(i, 1), :],
                                source[bass.ds(i, 1), q, :, :].rearrange("a d f -> d a f")).then_inc(S["w2_in"], 16)

        def finish_scalar(act):
            act.wait_ge(S["gap_done"], BATCH)
            act.activation(gap_exp[:, :], gap_all[:, :], ACT.Exp).then_inc(S["gap_exp_done"], 1)
            act.wait_ge(S["plan_done"], 1)
            zero_ends(act, mybir.EngineType.Activation, 1)
            def copy_rows(k, u):
                act.wait_ge(S["block_turned"], k + 1)
                act.copy(blockT[u % 4], turn_ps[u % 4]).then_inc(S["blockT_done"], 1)

            def silu(k, u):
                act.wait_ge(S["up_mm"], k + 1)
                wait(act, S["summed"], k - 1)
                act.activation(hidden[u % 2], up_ps[u % 4][:, :], ACT.Silu).then_inc(S["silu_done"], 1)

            for u in range(AHEAD):
                copy_rows(u, u)

            def turn_of_blocks(turn):
                for u in range(UNROLL):
                    if not isinstance(turn, int) or turn < TURNS - 1 or u < UNROLL - AHEAD:
                        copy_rows(UNROLL * turn + u + AHEAD, u + AHEAD)
                    silu(UNROLL * turn + u, u)

            run_turns(act, turn_of_blocks)
            for i, bank in enumerate((bank_a, bank_b)):
                act.wait_ge(S["gate_mm"], i + 1)
                act.copy(gateT_all[:, 4 * i:4 * i + 4, :].rearrange("p g t -> p (g t)"), bank[:, :]).then_inc(
                    S["gateT_done"], 1)

        def finish_vector(v):
            done = 0

            def link(ins):
                nonlocal done
                done += 1
                ins.then_inc(S["plan_dve"], 1)
                v.wait_ge(S["plan_dve"], done)

            v.wait_ge(S["count_mm"], 1)
            link(v.tensor_copy(counts[:, :], bank_c[:, 0:E]))
            v.tensor_tensor(end_i[:, :], counts[:, :], region[:, :], ALU.add).then_inc(S["plan_done"], 1)
            link(v.tensor_scalar(blocks_i[:, :], counts[:, :], float(P - 1), None, ALU.add))
            link(v.tensor_single_scalar(blocks_s[:, :], blocks_i[:, :], 7, ALU.arith_shift_right))
            link(v.tensor_copy(blocks[:, :], blocks_s[:, :]))
            link(v.tensor_tensor_scan(block_end[:, :], onesf[:, 0:E], blocks[:, :], 0.0, ALU.mult, ALU.add))
            wide = [P, 2, E]
            v.wait_ge(S["block_k_done"], 2)
            link(v.tensor_tensor(passed[:, :, :], block_end[:, :].unsqueeze(1).broadcast_to(wide),
                                 block_k[:, :].unsqueeze(2).broadcast_to(wide), ALU.is_le))
            link(v.tensor_reduce(plan_e[:, :], passed[:, :, :], AX.X, ALU.add))
            link(v.tensor_tensor(passed_blocks[:, :, :], passed[:, :, :],
                                 blocks[:, :].unsqueeze(1).broadcast_to(wide), ALU.mult))
            link(v.tensor_reduce(plan_b[:, :], passed_blocks[:, :, :], AX.X, ALU.add))
            link(v.tensor_tensor(plan_b[:, :], block_k[:, :], plan_b[:, :], ALU.subtract))
            link(v.tensor_scalar(plan_l[:, :], plan_e[:, :], float(E), float(P), ALU.is_lt, ALU.mult))
            link(v.tensor_tensor(plan_b[:, :], plan_b[:, :], plan_l[:, :], ALU.mult))
            link(v.scalar_tensor_tensor(out=plan_f[:, 0:2], in0=plan_e[:, :], scalar=float(CAP),
                                        in1=plan_b[:, :], op0=ALU.mult, op1=ALU.add))
            link(v.tensor_scalar(plan_f[:, 2:4], plan_e[:, :], float(E - 1), float(F), ALU.min, ALU.mult))
            v.sem_inc(S["plan_ready"], 1)
            v.wait_ge(S["plan_mm"], 1)
            v.tensor_copy(plan_i[:, :], bank_c[0:1, :]).then_inc(S["plan_done"], 1)
            v.wait_ge(S["gap_exp_done"], 1)
            v.wait_ge(S["chosen_kept"], BATCH)
            v.wait_ge(S["val_mm"], 2 * BATCH)
            link(v.tensor_scalar(gap_exp1[:, :], gap_exp[:, :], 1.0, None, ALU.add))
            link(v.reciprocal(share[:, 0, :], gap_exp1[:, :]))
            link(v.tensor_tensor(share[:, 1, :], gap_exp[:, :], share[:, 0, :], ALU.mult))
            for k in range(TOP_K):
                link(v.tensor_tensor(gates_k[:, k, :, :], chosen_all[:, k, :, :],
                                     share[:, k, :].unsqueeze(2).broadcast_to([P, TILES, E]), ALU.mult))
            v.tensor_tensor(gates[:, :, :], gates_k[:, 0, :, :], gates_k[:, 1, :, :], ALU.add).then_inc(
                S["gates_done"], 1)

            link(v.tensor_scalar(counts1[:, :], counts[:, :], 1.0, None, ALU.max))
            link(v.reciprocal(per_token[:, :], counts1[:, :]))
            link(v.tensor_reduce(d_of, ident[:, :].rearrange("p (q d) -> p d q", q=4), AX.X, ALU.add))
            link(v.tensor_reduce(quad_of, ident[:, :].rearrange("p (q d) -> p q d", q=4), AX.X, ALU.add))
            link(v.tensor_tensor(mean_of.rearrange("p (q g) -> p q g", q=4),
                                 per_token[:, :].rearrange("p (q g) -> p q g", q=4),
                                 quad_of.unsqueeze(2).broadcast_to([P, 4, 4]), ALU.mult))
            v.wait_ge(S["plan_done"], 2)
            v.wait_ge(S["sums_zero"], ZERO_PARTS)

            def add_hidden(turn):
                places = plan_values(DVE, 2 * P + UNROLL * turn, (E - 1) * F)
                for u, at in enumerate(places):
                    v.wait_ge(S["silu_done"], UNROLL * turn + u + 1)
                    wait(v, S["summed"], UNROLL * turn + u)
                    here = sums[:, bass.ds(at, F)]
                    v.tensor_tensor(here, here, hidden[u % 2], ALU.add).then_inc(S["summed"], 1)

            run_turns(v, add_hidden)
            v.wait_ge(S["w2_in"], 16 * 4 * E)
            for i in range(E):
                v.wait_ge(S["spread_mm"], i // 4 + 1)
                wait(v, S["y_done"], i - 1)
                v.tensor_tensor_reduce(y_prod[i % 2], up_ps[i // 4][:, :], w2_in_quads[:, i, :], 1.0, 0.0, ALU.mult,
                                       ALU.add, yT[:, i:i + 1]).then_inc(S["y_done"], 1)
            v.wait_ge(S["y_done"], E)
            for a in range(4):
                column = yT[:, :].rearrange("p (g a) -> p a g", a=4)[:, a, :]
                v.tensor_tensor(y_parts[:, a, :].rearrange("p (t q g) -> p t q g", t=8, q=4),
                                column.unsqueeze(1).unsqueeze(1).broadcast_to([P, 8, 4, 4]),
                                mean_of.rearrange("p (q g) -> p q g", q=4).unsqueeze(1).broadcast_to([P, 8, 4, 4]),
                                ALU.mult).then_inc(S["y_wide_done"], 1)
            v.wait_ge(S["y_mm"], 1)
            for half in range(2):
                tiles = slice(4 * half, 4 * half + 4)
                v.tensor_tensor(y_block[:, tiles, :], bank_c[:, 0:P].unsqueeze(1).broadcast_to([P, 4, D]),
                                tile_mask[:, tiles].unsqueeze(2).broadcast_to([P, 4, D]), ALU.mult).then_inc(
                    S["y_block_done"], 1)
            for i in range(TILES // 4):
                v.wait_ge(S["mix_mm"], i + 1)
                here = hres[:, 4 * i:4 * i + 4, :].rearrange("p t d -> p (t d)")
                v.tensor_tensor(here, here, up_ps[i % 4][:, :], ALU.add).then_inc(S["result_done"], 1)

        def finish_tensor(pe):
            pe.wait_ge(S["count_dve"], COUNT * BATCH)
            pe.wait_ge(S["slot_dve"], SLOT * BATCH)
            pe.matmul(bank_c[:, 0:E], onesb[:, :], before[BATCH % 2][:, 0, :], start=True, stop=True).then_inc(
                S["count_mm"], 1)
            pe.wait_ge(S["plan_ready"], 1)
            for c in range(4):
                mm = pe.transpose(bank_c[0:1, c * P:(c + 1) * P], plan_f[:, c:c + 1], ident[:, :])
            mm.then_inc(S["plan_mm"], 1)
            pe.wait_ge(S["v_done"], BATCH)
            pe.wait_ge(S["w1_done"], BATCH)
            pe.wait_ge(S["o_norm_done"], BATCH)
            pe.wait_ge(S["oT_done"], BATCH)
            pe.wait_ge(S["plan_done"], 2)
            pe.wait_ge(S["exp_done"], H * BATCH)

            def turn_rows(turn, u):
                pe.wait_ge(block_in[u], 16 * turn + 16)
                pe.transpose(turn_ps[u % 4], block_rows[u], ident[:, :]).then_inc(S["block_turned"], 1)

            def products(turn):
                places = plan_values(PE, 2 * P + UNROLL * turn, (E - 1) * F)
                for u in range(UNROLL):
                    k = UNROLL * turn + u
                    if u < UNROLL - AHEAD:
                        turn_rows(turn, u + AHEAD)
                    elif not isinstance(turn, int) or turn < TURNS - 1:
                        turn_rows(turn + 1, u + AHEAD - UNROLL)
                    at = next(places)
                    pe.wait_ge(S["blockT_done"], k + 1)
                    wait(pe, S["silu_done"], k - 3)
                    pe.matmul(up_ps[u % 4][:, :], blockT[u % 4], w1T[:, bass.ds(at, F)], start=True,
                              stop=True).then_inc(S["up_mm"], 1)

            for u in range(AHEAD):
                turn_rows(0, u)
            run_turns(pe, products)
            pe.wait_ge(S["gates_done"], 1)
            for g in range(8):
                mm = pe.transpose((bank_a, bank_b)[g // 4][:, (g % 4) * P:(g % 4 + 1) * P],
                                  gates[:, 8 * g:8 * g + 8, :].rearrange("p t e -> p (t e)"), ident[:, :])
                if g % 4 == 3:
                    mm.then_inc(S["gate_mm"], 1)
            pe.wait_ge(S["summed"], BLOCKS)
            for g in range(4):
                for q in range(4):
                    e = 4 * q + g
                    mm = pe.matmul(up_ps[g][QUAD * q:QUAD * (q + 1), :], onesf[:, 0:QUAD],
                                   sums[:, e * F:(e + 1) * F], start=True, stop=True)
                mm.then_inc(S["spread_mm"], 1)
            for a in range(4):
                pe.wait_ge(S["y_wide_done"], a + 1)
                mm = pe.matmul(bank_c[:, QUAD * a:QUAD * (a + 1)], y_parts[:, a, :], d_of, start=True, stop=True)
            mm.then_inc(S["y_mm"], 1)
            pe.wait_ge(S["gateT_done"], 2)
            for i in range(TILES // 4):
                if i < 2:
                    pe.wait_ge(S["y_block_done"], i + 1)
                wait(pe, S["result_done"], i - 3)
                pe.matmul(up_ps[i % 4][:, :], gateT_all[:, i // 2, :],
                          y_block[:, 4 * (i % 2):4 * (i % 2) + 4, :].rearrange("p t d -> p (t d)"), start=True,
                          stop=True).then_inc(S["mix_mm"], 1)

        block = ctx.enter_context(nc.Block())

        @block.sync
        def _(sp):
            sp.dma_start(w_nat[:, 0, :], wq).then_inc(S["weights_in"], 16)
            sp.dma_start(w_nat[:, 1, :], wk).then_inc(S["weights_in"], 16)
            sp.dma_start(w_nat[:, 2, :], wv).then_inc(S["weights_in"], 16)
            sp.dma_start(gate_nat[:, :], gate_w).then_inc(S["weights_in"], 16)
            sp.dma_start(emb_nat[:, :], emb).then_inc(S["weights_in"], 16)

            def shift_bias():
                sp.wait_ge(S["bias_row"], 3)
                sp.dma_start(bias_rows[:, :], bias_ext[:, :]).then_inc(S["bias_in"], 16)
                sp.wait_ge(S["bias_in"], 16)
                shifted = bass.AP(bias_rows, 0, [[1, P], [512, H], [1, BIASW]])
                sp.dma_start(probs[:, :, 0:BIASW], shifted).then_inc(S["bias_wide"], 16)

            def step(at):
                if written_out(at(0), BIAS_STEP - 1):
                    shift_bias()
                b = at(6)
                if b.live:
                    wait(sp, S["onehot_done"], b.n - 1)
                    row = x[bass.ds(b.n, 1), :]
                    sp.dma_start(tok[b.par][:, :], row.partition_broadcast(P)).then_inc(tok_in[b.par], 16)
                b = at(5)
                if b.live:
                    wait(sp, S["w1_mm"], b.n - 1)
                    rows = w1.rearrange("e f d -> (e f) d")[bass.ds(b.n * 2 * P, 2 * P), :]
                    sp.dma_start(w1_in[b.par][:, :, :], rows.rearrange("(t p) d -> p t d", p=P)).then_inc(
                        w1_loaded[b.par], 16)
                b = at(3)
                if b.live:
                    sp.wait_ge(S["split_pool"], b.n + 1)
                    wait(sp, S["scores_mm"], H * b.n - H)
                    for i, (pq, pk) in enumerate(TERMS):
                        for side, part in ((0, pq), (1, pk)):
                            sp.dma_start(stack[b.par][i * HD:(i + 1) * HD, side, :, :],
                                         qk_part[b.par][:, side, part, :]).then_inc(stacked[b.par], 16)

            run_steps(sp, step, LOOP_TO - 4)
            finish_sync(sp)

        @block.gpsimd
        def _(g):
            done = 0

            def tick(ins):
                nonlocal done
                done += 1
                ins.then_inc(S["const_pool"], 1)

            def made():
                g.wait_ge(S["const_pool"], done)

            tick(g.memset(ident[:, :], 0.0))
            tick(g.memset(identb[:, :], 0.0))
            tick(g.memset(anti[:, :], 0.0))
            tick(g.memset(group_mask[:, :], 1.0))
            made()
            diag = dict(compare_op=ALU.not_equal, fill=1.0, base=0, pattern=[[-1, P]], channel_multiplier=1)
            tick(g.affine_select(out=ident[:, :], in_=ident[:, :], **diag))
            tick(g.affine_select(out=identb[:, :], in_=identb[:, :], **diag))
            tick(g.affine_select(out=anti[:, :], in_=anti[:, :], compare_op=ALU.not_equal, fill=1.0,
                                 base=-(P - 1), pattern=[[1, P]], channel_multiplier=1))
            tick(g.affine_select(out=group_mask[:, :], in_=group_mask[:, :], compare_op=ALU.is_ge, fill=0.0,
                                 base=0, pattern=[[-GROUP, P // GROUP], [0, GROUP]], channel_multiplier=1))
            made()
            tick(g.affine_select(out=group_mask[:, :], in_=group_mask[:, :], compare_op=ALU.is_ge, fill=0.0,
                                 base=GROUP - 1, pattern=[[GROUP, P // GROUP], [0, GROUP]], channel_multiplier=-1))
            tick(g.iota(vocab_i[:, :], pattern=[[0, 1]], base=0, channel_multiplier=1))
            tick(g.iota(expert_i[:, :], pattern=[[1, E]], base=0, channel_multiplier=0))
            tick(g.memset(minus_half[:, :], -0.5))
            tick(g.memset(earlier[:, :], 1.0))
            tick(g.memset(minus_sel[:, :, :], 0.0))
            tick(g.memset(tile_mask[:, :], 1.0))
            made()
            tick(g.affine_select(out=minus_sel[:, :, :], in_=minus_sel[:, :, :], compare_op=ALU.not_equal,
                                 fill=-1.0, base=0, pattern=[[-1, H], [0, P]], channel_multiplier=1))
            tick(g.tensor_copy(vocab_f[:, :], vocab_i[:, :]))
            tick(g.tensor_copy(expert_f[:, :], expert_i[:, :]))
            tick(g.affine_select(out=earlier[:, :], in_=earlier[:, :], compare_op=ALU.is_gt, fill=0.0,
                                 base=0, pattern=[[1, P]], channel_multiplier=-1))
            tick(g.affine_select(out=tile_mask[:, :], in_=tile_mask[:, :], compare_op=ALU.is_ge, fill=0.0,
                                 base=0, pattern=[[-E, 8]], channel_multiplier=1))
            made()
            tick(g.affine_select(out=minus_sel[:, :, :], in_=minus_sel[:, :, :], compare_op=ALU.not_equal,
                                 fill=-1.0, base=-H, pattern=[[-1, H], [0, P]], channel_multiplier=1))
            tick(g.affine_select(out=tile_mask[:, :], in_=tile_mask[:, :], compare_op=ALU.is_ge, fill=0.0,
                                 base=E - 1, pattern=[[E, 8]], channel_multiplier=-1))
            tick(g.tensor_scalar(region[:, :], expert_f[:, :], float(CAP), None, ALU.mult))
            made()
            assert done == POOL_CONSTANTS
            g.wait_ge(S["const_dve"], DVE_CONSTANTS)
            g.dma_start(expert_rows[ZERO_ROW:ZERO_ROW + P, :], zeros[:, :]).then_inc(S["zero_row_out"], 16)

            def step(at):
                b = at(-3)
                if b.live:
                    g.wait_ge(S["slot_dve"], SLOT * b.n + SLOT)
                    for k in range(TOP_K):
                        for t in range(NT):
                            c = k * NT + t
                            settled(g, S["pool_passed"], b)
                            g.indirect_dma_start(expert_rows[0:ZERO_ROW, :],
                                                 bass.IndirectOffsetOnAxis(slot_i[b.par][:, c:c + 1], 0),
                                                 xn2[b.par][:, t, :], None).then_inc(scattered[b.par], 16)
                b = at(4)
                if b.live:
                    g.wait_ge(S["stat_dve"], STAT * b.n + STAT)
                    settled(g, S["pool_passed"], b)
                    g.tensor_scalar(var_eps[b.par][:, :], moments[b.par][:, :, 1], EPS, None, ALU.add).then_inc(
                        S["rstd_pool"], 1)
                    g.wait_ge(S["rstd_pool"], 2 * b.n + 1)
                    g.tensor_tensor(rstd[b.par][:, :], var_eps[b.par][:, :], minus_half[:, :], ALU.pow).then_inc(
                        S["rstd_pool"], 1)
                b = at(3)
                if b.live:
                    g.wait_ge(S["part2_done"], b.n + 1)
                    part = qk_part[b.par]
                    g.tensor_tensor(part[:, :, 2, :], qk_rest[b.par][:, :, :], part[:, :, 1, :],
                                    ALU.subtract).then_inc(S["split_pool"], 1)
                b = at(-2)
                if b.live:
                    g.wait_ge(S["route_dve"], ROUTE * b.n + ROUTE)
                    keep = chosen_all[:, :, bass.ds(NT * b.n, NT), :]
                    settled(g, S["pool_passed"], b)
                    g.tensor_copy(keep, chosen[b.par][:, :, :, :]).then_inc(S["chosen_kept"], 1)
                b = at(1)
                if b.live:
                    g.wait_ge(S["scored_dve"], NT * H * b.n + NT * H)
                    m, parts = row_max[b.par], max_parts[b.par]
                    settled(g, S["pool_passed"], b)
                    g.tensor_copy(parts[:, :, 0:H], m[:, :, :]).then_inc(S["max_split"], 1)
                    g.wait_ge(S["max_split"], 2 * b.n + 1)
                    g.tensor_tensor(parts[:, :, H:2 * H], m[:, :, :], parts[:, :, 0:H], ALU.subtract).then_inc(
                        S["max_split"], 1)
                b = at(-1)
                if b.live:
                    g.wait_ge(S["ln2_dve"], LN2 * b.n + LN2)
                    settled(g, S["pool_passed"], b)
                    g.tensor_scalar(var_eps2[:, :], moments2[:, :, 1], EPS, None, ALU.add).then_inc(S["rstd2_pool"], 1)
                    g.wait_ge(S["rstd2_pool"], RSTD2 * b.n + 1)
                    g.tensor_tensor(rstd2[:, :], var_eps2[:, :], minus_half[:, :], ALU.pow).then_inc(
                        S["rstd2_pool"], 1)
                b = at(1)
                if b.live:
                    g.tensor_scalar(minus_max[b.par][:, :, :], row_max[b.par][:, :, CENTERED_FROM:H], -1.0, None,
                                    ALU.mult).then_inc(S["minus_max_done"], 1)

            run_steps(g, step)
            finish_gpsimd(g)

        @block.scalar
        def _(act):
            act.dma_start(conv_nat[:, :, :], conv_w).then_inc(S["conv_in"], 16)
            with nc.allow_non_contiguous_dma(reason="a 4 KB table, once"):
                act.dma_start(bias_t[:, :], rel_bias[0].rearrange("h r -> r h")).then_inc(S["bias_t_in"], 16)

            def step(at):
                def bias_piece(i):
                    if written_out(at(0), BIAS_STEP):
                        act.wait_ge(S["bias_ps"], i + 1)
                        act.copy(bias_flat[:, i * 512:(i + 1) * 512], bias_banks[i][:, :]).then_inc(
                            S["bias_done"], 1)

                def center(b, h):
                    if b.live:
                        act.wait_ge(S["minus_max_done"], b.n + 1)
                        for t in range(NT):
                            part = scored[:, b.par, h, t * T:(t + 1) * T]
                            ins = act.activation(part, part, ACT.Identity,
                                                 bias=minus_max[b.par][:, t, h - CENTERED_FROM:h - CENTERED_FROM + 1])
                        ins.then_inc(S["centered"], 1)

                def exp(b, h):
                    if b.live:
                        act.wait_ge(S["turned_mm"], H * b.n + h + 1)
                        act.activation(probs[:, h, :], ps_turn[h % 2][:, :], ACT.Exp).then_inc(S["exp_done"], 1)

                exp(at(-1), 6)
                exp(at(-1), 7)
                b = at(0)
                if b.live:
                    act.wait_ge(S["max_mm"], b.n + 1)
                    act.copy(maxT[b.par][0:2 * H, :], max_ps).then_inc(S["maxT_done"], 1)
                b = at(4)
                if b.live:
                    if at(3).live:
                        act.wait_ge(S["xnT_mm"], at(3).n + 1)
                    else:
                        act.wait_ge(S["embed_mm"], b.n + 1)
                    h = hres[:, bass.ds(NT * b.n, NT), :].rearrange("p t d -> p (t d)")
                    act.activation(h, emb_ps, ACT.Relu).then_inc(S["relu_done"], 1)
                b = at(3)
                if b.live:
                    if not at(4).live:
                        act.wait_ge(S["xnT_mm"], b.n + 1)
                    act.copy(xnT[b.par][:, :], xnT_ps).then_inc(S["xnT_done"], 1)
                exp(at(0), 0)
                center(at(0), CENTERED_FROM + 0)
                b = at(3)
                if b.live:
                    act.wait_ge(S["qk_mm"], b.n + 1)
                    act.copy(qk_part[b.par][:, :, 0, :], qk_ps.rearrange("p (s t) -> p s t", s=2)).then_inc(
                        S["part1_done"], 1)
                b = at(-2)
                if b.live:
                    act.wait_ge(S["xn2T_mm"], b.n + 1)
                    act.copy(xn2T[:, :], xn2T_ps).then_inc(S["xn2T_done"], 1)
                b = at(-1)
                if b.live:
                    act.wait_ge(S["val_mm"], 2 * b.n + 2)
                    act.copy(oT[:, :], ps_val[:, :]).then_inc(S["oT_done"], 1)
                exp(at(0), 1)
                center(at(0), CENTERED_FROM + 1)
                bias_piece(1)
                if written_out(at(0), BATCH):
                    zero_sums(act, 5, ZERO_PARTS)
                b = at(4)
                if b.live:
                    act.wait_ge(S["w1_mm"], b.n + 1)
                    act.copy(w1T[:, bass.ds(2 * P * b.n, 2 * P)], w1_ps).then_inc(S["w1_done"], 1)
                exp(at(0), 2)
                center(at(0), CENTERED_FROM + 2)
                exp(at(0), 3)
                center(at(0), CENTERED_FROM + 3)
                bias_piece(3)
                b = at(3)
                if b.live:
                    act.wait_ge(S["rest_done"], b.n + 1)
                    act.copy(qk_part[b.par][:, :, 1, :], qk_rest[b.par][:, :, :]).then_inc(S["part2_done"], 1)
                b = at(3)
                if b.live:
                    act.wait_ge(S["v_mm"], b.n + 1)
                    act.copy(v_op[b.quarter][:, :, :, 0:HD],
                             v_ps.rearrange("p (t h d) -> p t h d", t=NT, d=HD)).then_inc(S["v_done"], 1)
                exp(at(0), 4)
                exp(at(0), 5)
                bias_piece(5)

            run_steps(act, step)
            finish_scalar(act)

        @block.vector
        def _(v):
            v.memset(zeros[:, :], 0.0).then_inc(S["const_dve"], 1)
            v.memset(onesf[:, :], 1.0).then_inc(S["const_dve"], 1)
            v.memset(onesb[:, :], 1.0).then_inc(S["const_dve"], 1)
            for i in range(4):
                v.memset(v_op[i][:, :, :, HD + 1:VW], 0.0).then_inc(S["const_dve"], 1)
                v.memset(v_op[i][:, :, :, HD:HD + 1], 1.0).then_inc(S["const_dve"], 1)
            for i in range(2):
                v.memset(maxT[i][:, :], 0.0).then_inc(S["const_dve"], 1)
                v.memset(onehot[i][:, 0:1], 0.0).then_inc(S["const_dve"], 1)
            v.memset(before[0][:, 0, :], 0.0).then_inc(S["const_dve"], 1)
            v.wait_ge(S["conv_in"], 16)
            v.wait_ge(S["const_pool"], GROUPS_MADE)
            for k in range(CONTEXT):
                tap = conv_nat[:, :, k].unsqueeze(1).broadcast_to([P, P // GROUP, GROUP])
                v.tensor_tensor(conv_wide[:, k, :].rearrange("p (g c) -> p g c", c=GROUP),
                                group_mask[:, :].rearrange("p (g c) -> p g c", c=GROUP), tap, ALU.mult).then_inc(
                    S["setup_dve"], 1)
            v.wait_ge(S["setup_pe"], 1)
            for i in range(2):
                v.tensor_scalar(wqkT[:, i, :].rearrange("p (d h) -> p d h", h=H),
                                bank_a[:, i * P:(i + 1) * P].rearrange("p (h d) -> p d h", h=H),
                                HD ** -0.5 if i == 0 else 1.0, None, ALU.mult).then_inc(S["setup_dve"], 1)
            v.tensor_copy(wvT[:, :], bank_a[:, 2 * P:3 * P]).then_inc(S["setup_dve"], 1)
            v.tensor_copy(gateT[:, :], bank_a[:, 3 * P:3 * P + E]).then_inc(S["setup_dve"], 1)
            v.tensor_copy(embT[:, :], bank_b[:, 0:VOCAB]).then_inc(S["setup_dve"], 1)
            v.tensor_copy(convT[:, :, :], bank_b[:, P:3 * P].rearrange("p (k o) -> p k o", k=CONTEXT)).then_inc(
                S["setup_dve"], 1)
            v.wait_ge(S["setup_pe"], 2)
            rev = bank_c[0:H, 2 * D:2 * D + NREL]
            lead = 2 * P - WINDOW
            v.tensor_copy(bias_ext[:, lead:lead + NREL], rev).then_inc(S["bias_row"], 1)
            v.tensor_copy(bias_ext[:, 0:lead], rev[:, 0:1].broadcast_to([H, lead])).then_inc(S["bias_row"], 1)
            tail = 512 - lead - NREL
            v.tensor_copy(bias_ext[:, 512 - tail:512], rev[:, NREL - 1:NREL].broadcast_to([H, tail])).then_inc(
                S["bias_row"], 1)
            product = bank_c[0:VOCAB, 0:2 * D].rearrange("p (k o) -> p k o", k=CONTEXT)
            rest = table_rest[0:VOCAB, :, :]
            v.tensor_copy(table[0:VOCAB, 0, :, :], product).then_inc(S["table_done"], 1)
            v.wait_ge(S["table_done"], 1)
            v.tensor_tensor(rest, product, table[0:VOCAB, 0, :, :], ALU.subtract).then_inc(S["table_done"], 1)
            v.wait_ge(S["table_done"], 2)
            v.tensor_copy(table[0:VOCAB, 1, :, :], rest).then_inc(S["table_done"], 1)
            v.wait_ge(S["table_done"], 3)
            v.tensor_tensor(table[0:VOCAB, 2, :, :], rest, table[0:VOCAB, 1, :, :], ALU.subtract).then_inc(
                S["table_done"], 1)
            v.wait_ge(S["const_pool"], POOL_CONSTANTS)
            for c in range(2):
                v.tensor_scalar(block_k[:, c:c + 1], vocab_f[:, :], float(P * c), None, ALU.add).then_inc(
                    S["block_k_done"], 1)

            def step(at):
                def bias_piece(i):
                    if written_out(at(0), BIAS_STEP):
                        v.wait_ge(S["bias_ps"], i + 1)
                        v.tensor_copy(bias_flat[:, i * 512:(i + 1) * 512], bias_banks[i][:, :]).then_inc(
                            S["bias_done"], 1)

                def score(h, t):
                    b = at(1)
                    if b.live:
                        if t == 0:
                            v.wait_ge(S["scores_mm"], H * b.n + h + 1)
                            settled(v, S["vector_passed"], b)
                        u = P - P * t
                        v.tensor_tensor_reduce(scored[:, b.par, h, t * T:(t + 1) * T],
                                               ps_score[h % 2][:, t * T:(t + 1) * T], bias[:, h, u:u + T],
                                               1.0, LOW, ALU.add, ALU.max,
                                               row_max[b.par][:, t, h:h + 1]).then_inc(S["scored_dve"], 1)

                def tile_of(b, t):
                    return hres[:, bass.ds(NT * b.n + t, 1), :].rearrange("p t d -> p (t d)")

                if written_out(at(1), 0):
                    v.wait_ge(S["bias_done"], 6)
                score(0, 0)
                place(v, at(-3), 0)
                score(0, 1)
                place(v, at(-3), 1)
                b = at(-2)
                if b.live:
                    v.wait_ge(S["rstd2_pool"], RSTD2 * b.n + RSTD2)
                    wait(v, scattered[b.par], 16 * TOP_K * NT * b.half)
                    for t in range(NT):
                        v.tensor_scalar(xn2[b.par][:, t, :], tile_of(b, t), moments2[:, t, 0:1],
                                        rstd2[:, t:t + 1], ALU.subtract, ALU.mult).then_inc(S["xn2_done"], 1)
                score(1, 0)
                place(v, at(-3), 2)
                score(1, 1)
                place(v, at(-3), 3)
                score(2, 0)
                score(2, 1)
                b = at(5)
                if b.live:
                    v.wait_ge(tok_in[b.par], 16 * b.half + 16)
                    v.tensor_scalar(onehot[b.par][:, 1:1 + T], tok[b.par][:, :], float(VOCAB - 1), vocab_f[:, 0:1],
                                    ALU.min, ALU.is_equal).then_inc(S["onehot_done"], 1)
                b = at(3)
                if b.live:
                    v.wait_ge(S["part1_done"], b.n + 1)
                    v.tensor_tensor(qk_rest[b.par][:, :, :], qk_ps.rearrange("p (s t) -> p s t", s=2),
                                    qk_part[b.par][:, :, 0, :], ALU.subtract).then_inc(S["rest_done"], 1)
                if written_out(at(0), BATCH + 1):
                    zero_sums(v, 0, 5)
                score(3, 0)
                b = at(4)
                if b.live:
                    v.wait_ge(S["relu_done"], b.n + 1)
                    settled(v, S["vector_passed"], b)
                    for t in range(NT):
                        v.bn_stats(stats[b.par][:, t, :], tile_of(b, t)).then_inc(S["stat_dve"], 1)
                score(3, 1)
                if b.live:
                    v.wait_ge(S["stat_dve"], STAT * b.n + NT)
                    settled(v, S["vector_passed"], b)
                    for t in range(NT):
                        v.bn_aggr(moments[b.par][:, t, :], stats[b.par][:, t, :]).then_inc(S["stat_dve"], 1)
                score(4, 0)
                bias_piece(0)
                score(4, 1)
                route_logits(v, at(-2))
                score(5, 0)
                route_largest(v, at(-2))
                if b.live:
                    v.wait_ge(S["rstd_pool"], 2 * b.n + 2)
                    for t in range(NT):
                        v.tensor_scalar(xn[b.par][:, t, :], tile_of(b, t), moments[b.par][:, t, 0:1],
                                        rstd[b.par][:, t:t + 1], ALU.subtract, ALU.mult).then_inc(S["xn_done"], 1)
                bias_piece(2)
                route_index(v, at(-2))
                score(5, 1)
                route_choice(v, at(-2))
                b = at(-1)
                if b.live:
                    v.wait_ge(S["o_mm"], b.n + 1)
                    o = o_ps.rearrange("p (c w) -> p c w", w=VW)
                    v.reciprocal(o_rec[:, :].unsqueeze(2), o[:, :, HD:HD + 1]).then_inc(S["o_chain"], 1)
                score(6, 0)
                route_mask(v, at(-2))
                if b.live:
                    v.wait_ge(S["o_chain"], b.n + 1)
                    v.tensor_tensor(o_norm[:, :, :].rearrange("p t (h d) -> p (t h) d", d=HD), o[:, :, 0:HD],
                                    o_rec[:, :].unsqueeze(2).broadcast_to([P, NT * H, HD]), ALU.mult).then_inc(
                        S["o_norm_done"], 1)
                score(6, 1)
                route_count(v, at(-2), 0)
                if b.live:
                    v.wait_ge(S["o_norm_done"], b.n + 1)
                    h = hres[:, bass.ds(NT * b.n, NT), :]
                    v.tensor_tensor(h, h, o_norm[:, :, :], ALU.add).then_inc(S["hres_done"], 1)
                bias_piece(4)
                score(7, 0)
                score(7, 1)
                route_count(v, at(-2), 1)
                if b.live:
                    v.wait_ge(S["hres_done"], b.n + 1)
                    settled(v, S["vector_passed"], b)
                    for t in range(NT):
                        v.bn_stats(stats2[:, t, :], tile_of(b, t)).then_inc(S["ln2_dve"], 1)
                if b.live:
                    v.wait_ge(S["ln2_dve"], LN2 * b.n + NT)
                    settled(v, S["vector_passed"], b)
                    for t in range(NT):
                        v.bn_aggr(moments2[:, t, :], stats2[:, t, :]).then_inc(S["ln2_dve"], 1)

            run_steps(v, step, LOOP_TO - 4)
            finish_vector(v)

        @block.tensor
        def _(pe):
            pe.wait_ge(S["const_pool"], IDENT_MADE)
            pe.wait_ge(S["weights_in"], 80)
            for i in range(3):
                pe.transpose(bank_a[:, i * P:(i + 1) * P], w_nat[:, i, :], ident[:, :])
            pe.transpose(bank_a[:, 3 * P:3 * P + E], gate_nat[:, :], ident[0:E, 0:E])
            pe.transpose(bank_b[:, 0:VOCAB], emb_nat[:, :], ident[0:VOCAB, 0:VOCAB])
            pe.wait_ge(S["setup_dve"], CONTEXT)
            for k in range(CONTEXT):
                mm = pe.transpose(bank_b[:, (k + 1) * P:(k + 2) * P], conv_wide[:, k, :], ident[:, :])
            mm.then_inc(S["setup_pe"], 1)
            pe.wait_ge(S["setup_dve"], CONTEXT + 6)
            for k in range(CONTEXT):
                pe.matmul(bank_c[0:VOCAB, k * D:(k + 1) * D], embT[:, :], convT[:, k, :], start=True, stop=True)
            pe.wait_ge(S["bias_t_in"], 16)
            pe.matmul(bank_c[0:H, 2 * D:2 * D + NREL], bias_t[:, :], anti[0:NREL, 1:P], start=True,
                      stop=True).then_inc(S["setup_pe"], 1)
            pe.wait_ge(S["table_done"], 4)
            pe.wait_ge(S["const_pool"], POOL_CONSTANTS)
            pe.wait_ge(S["const_dve"], DVE_CONSTANTS)

            def step(at):
                def bias_piece(i):
                    if not written_out(at(0), BIAS_STEP):
                        return
                    pe.wait_ge(S["bias_wide"], 16)
                    pe.wait_ge(S["bias_row"], 3)
                    h, u = divmod(i * 512, BIASW)
                    done = 0
                    while done < 512:
                        n = min(BIASW - u, 512 - done)
                        mm = pe.matmul(bias_banks[i][:, done:done + n], anti[:, :], probs[:, h, u:u + n],
                                       start=True, stop=True)
                        done, u, h = done + n, 0, h + 1
                    mm.then_inc(S["bias_ps"], 1)

                def score(h):
                    b = at(1)
                    if b.live:
                        if h == 0:
                            pe.wait_ge(stacked[b.par], 32 * len(TERMS) * b.half + 32 * len(TERMS))
                        wait(pe, S["scored_dve"], NT * (H * b.n + h - 1))
                        st = stack[b.par]
                        for t in range(NT):
                            mm = pe.matmul(ps_score[h % 2][:, t * T:(t + 1) * T], st[:, 0, h, t * P:(t + 1) * P],
                                           st[:, 1, h, :], start=True, stop=True)
                        mm.then_inc(S["scores_mm"], 1)

                def turn(b, h):
                    if not b.live:
                        return
                    wait(pe, S["exp_done"], H * b.n + h - 1)
                    if h >= CENTERED_FROM:
                        pe.wait_ge(S["centered"], CENTERED * b.n + h - CENTERED_FROM + 1)
                    bank = ps_turn[h % 2]
                    for j in range(NT):
                        for t in range(NT):
                            mm = pe.matmul(bank[:, j * T + t * P:j * T + (t + 1) * P],
                                           scored[:, b.par, h, t * T + j * P:t * T + (j + 1) * P], ident[:, :],
                                           start=(j + t == 0), stop=(h >= CENTERED_FROM and j + t == 2 * NT - 2),
                                           is_transpose=True, skip_group_check=True)
                    if h < CENTERED_FROM:
                        if h == 0:
                            pe.wait_ge(S["maxT_done"], b.n + 1)
                        mm = pe.matmul(bank[:, :].rearrange("p (j t) -> p j t", j=NT), minus_sel[:, h, :],
                                       maxT[b.par][:, :].unsqueeze(1).broadcast_to([P, NT, T]),
                                       start=False, stop=True, skip_group_check=True)
                    mm.then_inc(S["turned_mm"], 1)

                def values(b, group):
                    if not b.live:
                        return
                    pe.wait_ge(S["exp_done"], H * b.n + 4 * group + 4)
                    if group == 0:
                        wait(pe, S["oT_done"], b.n)
                    for j in range(NT):
                        for q in range(4):
                            h = 4 * group + q
                            mm = pe.matmul(ps_val[VW * q:VW * (q + 1), group * T:(group + 1) * T],
                                           v_op[b.quarter][:, j, h, :], probs[:, h, j * T:(j + 1) * T],
                                           start=(j == 0), stop=(j == NT - 1))
                    mm.then_inc(S["val_mm"], 1)

                if written_out(at(1), 0):
                    pe.wait_ge(S["bias_done"], 6)
                score(0)
                turn(at(-1), 6)
                score(1)
                turn(at(-1), 7)
                b = at(4)
                if b.live:
                    pe.wait_ge(S["onehot_done"], b.n + 1)
                    if at(2).live:
                        pe.wait_ge(S["v_done"], at(2).n + 1)
                    else:
                        wait(pe, S["w1_done"], b.n)
                    for t in range(NT):
                        for k in range(CONTEXT):
                            for part in range(3):
                                mm = pe.matmul(emb_ps[:, t * D:(t + 1) * D],
                                               onehot[b.par][0:VOCAB, t * P + k:t * P + k + P],
                                               table[0:VOCAB, part, k, :], start=(k == 0 and part == 0),
                                               stop=(k == CONTEXT - 1 and part == 2))
                    mm.then_inc(S["embed_mm"], 1)
                b = at(3)
                if b.live:
                    pe.wait_ge(S["xn_done"], NT * b.n + NT)
                    if not at(4).live:
                        wait(pe, S["v_done"], b.n)
                    for t in range(NT):
                        mm = pe.transpose(xnT_ps[:, t * P:(t + 1) * P], xn[b.par][:, t, :], ident[:, :])
                    mm.then_inc(S["xnT_mm"], 1)
                b = at(0)
                if b.live:
                    pe.wait_ge(S["max_split"], 2 * b.n + 2)
                    if at(-3).live:
                        wait(pe, S["slot_dve"], SLOT * at(-3).n + 1)
                    for t in range(NT):
                        mm = pe.transpose(max_ps[:, t * P:(t + 1) * P], max_parts[b.par][:, t, :], identb[:, :])
                    mm.then_inc(S["max_mm"], 1)
                bias_piece(0)
                score(2)
                turn(at(0), 0)
                b = at(-2)
                if b.live:
                    pe.wait_ge(S["xn2_done"], NT * b.n + NT)
                    if not at(0).live and at(-3).live:
                        pe.wait_ge(S["slot_dve"], SLOT * at(-3).n + 1)
                    for t in range(NT):
                        mm = pe.transpose(xn2T_ps[:, t * P:(t + 1) * P], xn2[b.par][:, t, :], ident[:, :])
                    mm.then_inc(S["xn2T_mm"], 1)
                b = at(3)
                if b.live:
                    pe.wait_ge(S["xnT_done"], b.n + 1)
                    prev = at(-2)
                    if prev.live:
                        pe.wait_ge(S["o_norm_done"], prev.n + 1)
                    for side in range(2):
                        mm = pe.matmul(qk_ps[:, side * T:(side + 1) * T], wqkT[:, side, :], xnT[b.par][:, :],
                                       start=True, stop=True)
                    mm.then_inc(S["qk_mm"], 1)
                bias_piece(1)
                values(at(-1), 1)
                score(3)
                turn(at(0), 1)
                b = at(-2)
                if b.live:
                    pe.wait_ge(S["xn2T_done"], b.n + 1)
                    for t in range(NT):
                        mm = pe.matmul(logit_ps[:, t * E:(t + 1) * E], xn2T[:, t * P:(t + 1) * P], gateT[:, :],
                                       start=True, stop=True)
                    mm.then_inc(S["logit_mm"], 1)
                bias_piece(2)
                b = at(4)
                if b.live:
                    pe.wait_ge(w1_loaded[b.par], 16 * b.half + 16)
                    if not at(3).live:
                        pe.wait_ge(S["relu_done"], b.n + 1)
                    for t in range(2):
                        mm = pe.transpose(w1_ps[:, t * P:(t + 1) * P], w1_in[b.par][:, t, :], ident[:, :])
                    mm.then_inc(S["w1_mm"], 1)
                score(4)
                turn(at(0), 2)
                bias_piece(3)
                b = at(-1)
                if b.live:
                    pe.wait_ge(S["oT_done"], b.n + 1)
                    other = at(3)
                    if other.live:
                        pe.wait_ge(S["rest_done"], other.n + 1)
                    for t in range(NT):
                        for group in range(2):
                            c = t * 2 + group
                            mm = pe.transpose(o_ps[:, c * P:(c + 1) * P],
                                              oT[:, group * T + t * P:group * T + (t + 1) * P], ident[:, :])
                    mm.then_inc(S["o_mm"], 1)
                score(5)
                turn(at(0), 3)
                bias_piece(4)
                b = at(3)
                if b.live:
                    other = at(4)
                    if other.live:
                        pe.wait_ge(S["w1_done"], other.n + 1)
                    for t in range(NT):
                        mm = pe.matmul(v_ps[:, t * D:(t + 1) * D], xnT[b.par][:, t * P:(t + 1) * P], wvT[:, :],
                                       start=True, stop=True)
                    mm.then_inc(S["v_mm"], 1)
                score(6)
                turn(at(0), 4)
                bias_piece(5)
                score(7)
                turn(at(0), 5)
                values(at(0), 0)
                b = at(-2)
                if b.live:
                    pe.wait_ge(S["count_dve"], COUNT * b.n + 1)
                    for t in range(NT):
                        pe.matmul(rank_ps[:, t * E:(t + 1) * E], earlier[:, :], mask[b.par][:, t, :],
                                  start=True, stop=False)
                        mm = pe.matmul(rank_ps[:, t * E:(t + 1) * E], onesb[:, :], before[b.par][:, t, :],
                                       start=False, stop=True)
                    mm.then_inc(S["rank_mm"], 1)

            run_steps(pe, step)
            finish_tensor(pe)


_INS = ["x", "L0_tok_emb_table", "L0_tok_conv_w", "L0_attn_Wq", "L0_attn_Wk", "L0_attn_Wv", "L0_attn_rel_pos_bias",
        "L0_ffn_gate_weight", "L0_ffn_w1", "L0_ffn_w2"]


def kernel(**inputs):
    import numpy as _np
    import concourse.bacc as _bacc
    from concourse import mybir as _mybir
    from concourse.bass_utils import run_bass_kernel_spmd as _run

    nc = _bacc.Bacc("TRN2", target_bir_lowering=False, num_devices=1)
    arrays, args = {}, []
    for name in _INS:
        a = _np.ascontiguousarray(inputs[name])
        arrays[f"in_{name}"] = a
        args.append(nc.dram_tensor(f"in_{name}", a.shape, _mybir.dt.from_np(a.dtype), kind="ExternalInput").ap())
    out = nc.dram_tensor("out_0", (BATCH, T, D), _mybir.dt.float32, kind="ExternalOutput").ap()
    tower_kernel(nc, *args, out)
    r = _run(nc, [arrays], core_ids=[0])
    return r.results[0]["out_0"]
```
